# Optimizing a Trainium2 kernel written in Bass

```python
import numpy as np
import jax
import jax.numpy as jnp

def _softmax(x, axis=-1):
    return jax.nn.softmax(x, axis=axis)

def _gelu(x):
    return jax.nn.gelu(x, approximate=True)

def _silu(x):
    return jax.nn.silu(x)

def _sigmoid(x):
    return jax.nn.sigmoid(x)

def _layernorm(x, axis=-1, eps=1e-05):
    m = jnp.mean(x, axis=axis, keepdims=True)
    v = jnp.var(x, axis=axis, keepdims=True)
    return (x - m) / jnp.sqrt(v + eps)

def _scatter_add(tgt, idx, src, axis=0):
    return tgt.at[idx].add(src)

def _segment_sum(src, seg, n):
    return jax.ops.segment_sum(src, seg, n)
kernel_name = 'mk_xattn_ffn_d1_seqx_r8_ebe065'

def setup_inputs(seed: int=0):
    np.random.seed(seed)
    _w = jnp.asarray

    def _rec_inputs():
        import jax
        import jax.numpy as jnp
        _rk = jax.random.key(seed)
        x = -0.0005146 + 1 * jax.random.normal(jax.random.fold_in(_rk, 1), (4, 512, 128), jnp.float32)
        _lenS = 512 - jax.random.randint(jax.random.fold_in(_rk, 7), (4,), 0, max(1, 512 // 4) + 1, jnp.int32)
        _lenS2 = 77 - jax.random.randint(jax.random.fold_in(_rk, 8), (4,), 0, max(1, 77 // 4) + 1, jnp.int32)
        _ctx_768P = jax.random.normal(jax.random.fold_in(_rk, 11), (4, 16, 96), jnp.float32)
        _ctx_768c = jax.random.dirichlet(jax.random.fold_in(_rk, 511), 0.3 * jnp.ones((16,), jnp.float32), (4, 77))
        _ctx_768t = jnp.einsum('bsk,bkd->bsd', _ctx_768c, _ctx_768P)
        _ctx_768t = _ctx_768t * jax.lax.rsqrt(jnp.mean(jnp.square(_ctx_768t)) + 1e-12) * 0.953939
        ctx_768 = -0.00040386 + 0.999972 * (_ctx_768t + 0.3 * jax.random.normal(jax.random.fold_in(_rk, 611), (4, 77, 96), jnp.float32))
        _validS = jnp.arange(512)[None, :] < _lenS[:, None]
        _validS2 = jnp.arange(77)[None, :] < _lenS2[:, None]
        _causal = jnp.tril(jnp.ones((512, 512), dtype=bool))
        mask_BxS2_bk0 = jnp.logical_not(jnp.broadcast_to(_validS2[:, :], (4, 77)))
        return (x, ctx_768, mask_BxS2_bk0)
    x, ctx_768, mask_BxS2_bk0 = _rec_inputs()

    def _L0_xattn_setup():
        import jax, jax.numpy as jnp
        import numpy as np
        DIM_IN, DIM_LAT, DIM_HEAD = (96, 128, 64)
        INNER = max(DIM_LAT, DIM_IN)
        HEADS = INNER // DIM_HEAD
        SCALE = DIM_HEAD ** (-0.5)
        RMS_EPS = 1e-08
        LN_EPS = 1e-05

        def layernorm(x, g, b):
            mu = jnp.mean(x, axis=-1, keepdims=True)
            var = jnp.mean((x - mu) ** 2, axis=-1, keepdims=True)
            return (x - mu) * jax.lax.rsqrt(var + LN_EPS) * g + b

        def rmsnorm(x, gamma):
            norm = jnp.sqrt(jnp.sum(x * x, axis=-1, keepdims=True)) * x.shape[-1] ** (-0.5)
            return x / jnp.maximum(norm, RMS_EPS) * gamma
        key = jax.random.key(seed)
        ks = jax.random.split(key, 12)
        b, n, m = (4, 512, 64)
        x = jax.random.normal(ks[0], (b, n, DIM_IN), jnp.float32)
        latents = jax.random.normal(ks[1], (b, m, DIM_LAT), jnp.float32)
        mask = jax.random.randint(ks[2], (b, n), 0, 2).astype(bool)
        s = lambda k, sh, fan: jax.random.normal(k, sh, jnp.float32) * fan ** (-0.5)
        return {'x': x, 'latents': latents, 'mask': mask, 'ln_x_g': jnp.ones((DIM_IN,), jnp.float32), 'ln_x_b': jnp.zeros((DIM_IN,), jnp.float32), 'ln_l_g': jnp.ones((DIM_LAT,), jnp.float32), 'ln_l_b': jnp.zeros((DIM_LAT,), jnp.float32), 'qn_g': jnp.ones((DIM_HEAD,), jnp.float32), 'kn_g': jnp.ones((DIM_HEAD,), jnp.float32), 'Wq': s(ks[3], (INNER, DIM_LAT), DIM_LAT), 'Wkv': s(ks[4], (2 * INNER, DIM_IN), DIM_IN), 'Wlkv': s(ks[5], (2 * INNER, DIM_LAT), DIM_LAT), 'Wo': s(ks[6], (DIM_LAT, INNER), INNER), 'bo': jnp.zeros((DIM_LAT,), jnp.float32)}
    _L0_xattn_all = _L0_xattn_setup()
    _L0_xattn_in = {k: v for k, v in _L0_xattn_all.items() if k in ('ln_x_g', 'ln_x_b', 'ln_l_g', 'ln_l_b', 'qn_g', 'kn_g', 'Wq', 'Wkv', 'Wlkv', 'Wo', 'bo')}
    del _L0_xattn_all

    def _L0_ffn_setup():
        import jax, jax.numpy as jnp
        import numpy as np
        B, S, H, E, K = (4, 256, 128, 8, 2)
        key = jax.random.key(seed)
        kx, kw, kb, kg, kgb = jax.random.split(key, 5)
        scale = 1.0 / np.sqrt(H)
        return {'x': jax.random.normal(kx, (B, S, H), dtype=jnp.float32), 'W': jax.random.normal(kw, (E, H, H), dtype=jnp.float32) * scale, 'b': jax.random.normal(kb, (E, H), dtype=jnp.float32) * scale, 'Wg': jax.random.normal(kg, (H, E), dtype=jnp.float32) * scale, 'bg': jax.random.normal(kgb, (E,), dtype=jnp.float32) * scale}
    _L0_ffn_all = _L0_ffn_setup()
    _L0_ffn_in = {k: v for k, v in _L0_ffn_all.items() if k in ('W', 'b', 'Wg', 'bg')}
    del _L0_ffn_all
    return {'x': x, 'ctx_768': ctx_768, 'mask_BxS2_bk0': mask_BxS2_bk0, 'L0_xattn_ln_x_g': _L0_xattn_in['ln_x_g'], 'L0_xattn_ln_x_b': _L0_xattn_in['ln_x_b'], 'L0_xattn_ln_l_g': _L0_xattn_in['ln_l_g'], 'L0_xattn_ln_l_b': _L0_xattn_in['ln_l_b'], 'L0_xattn_qn_g': _L0_xattn_in['qn_g'], 'L0_xattn_kn_g': _L0_xattn_in['kn_g'], 'L0_xattn_Wq': _L0_xattn_in['Wq'], 'L0_xattn_Wkv': _L0_xattn_in['Wkv'], 'L0_xattn_Wlkv': _L0_xattn_in['Wlkv'], 'L0_xattn_Wo': _L0_xattn_in['Wo'], 'L0_xattn_bo': _L0_xattn_in['bo'], 'L0_ffn_W': _L0_ffn_in['W'], 'L0_ffn_b': _L0_ffn_in['b'], 'L0_ffn_Wg': _L0_ffn_in['Wg'], 'L0_ffn_bg': _L0_ffn_in['bg']}

def reference(x, ctx_768, mask_BxS2_bk0, L0_xattn_ln_x_g, L0_xattn_ln_x_b, L0_xattn_ln_l_g, L0_xattn_ln_l_b, L0_xattn_qn_g, L0_xattn_kn_g, L0_xattn_Wq, L0_xattn_Wkv, L0_xattn_Wlkv, L0_xattn_Wo, L0_xattn_bo, L0_ffn_W, L0_ffn_b, L0_ffn_Wg, L0_ffn_bg):
    import jax
    import jax.numpy as jnp

    def _L0_xattn_ref(x, latents, mask, ln_x_g, ln_x_b, ln_l_g, ln_l_b, qn_g, kn_g, Wq, Wkv, Wlkv, Wo, bo):
        import jax, jax.numpy as jnp
        import numpy as np
        DIM_IN, DIM_LAT, DIM_HEAD = (96, 128, 64)
        INNER = max(DIM_LAT, DIM_IN)
        HEADS = INNER // DIM_HEAD
        SCALE = DIM_HEAD ** (-0.5)
        RMS_EPS = 1e-08
        LN_EPS = 1e-05

        def layernorm(x, g, b):
            mu = jnp.mean(x, axis=-1, keepdims=True)
            var = jnp.mean((x - mu) ** 2, axis=-1, keepdims=True)
            return (x - mu) * jax.lax.rsqrt(var + LN_EPS) * g + b

        def rmsnorm(x, gamma):
            norm = jnp.sqrt(jnp.sum(x * x, axis=-1, keepdims=True)) * x.shape[-1] ** (-0.5)
            return x / jnp.maximum(norm, RMS_EPS) * gamma
        b, n, _ = x.shape
        m = latents.shape[1]
        xn = layernorm(x, ln_x_g, ln_x_b)
        ln = layernorm(latents, ln_l_g, ln_l_b)
        q = ln @ Wq.T
        kv = jnp.concatenate([xn @ Wkv.T, ln @ Wlkv.T], axis=1)
        k, v = (kv[..., :INNER], kv[..., INNER:])
        split_heads = lambda t: t.reshape(t.shape[0], t.shape[1], HEADS, DIM_HEAD).transpose(0, 2, 1, 3)
        q, k, v = (split_heads(q), split_heads(k), split_heads(v))
        qn = rmsnorm(q, qn_g) * SCALE
        kn = rmsnorm(k, kn_g)
        attn = jnp.einsum('bhid,bhjd->bhij', qn, kn)
        full_mask = jnp.pad(mask, ((0, 0), (0, m)), constant_values=True)
        attn = jnp.where(full_mask[:, None, None, :], attn, -jnp.finfo(attn.dtype).max)
        attn = jax.nn.softmax(attn, axis=-1)
        out = jnp.einsum('bhij,bhjd->bhid', attn, v)
        out = out.transpose(0, 2, 1, 3).reshape(b, m, INNER)
        return out @ Wo.T + bo

    def _L0_ffn_ref(x, W, b, Wg, bg):
        import jax, jax.numpy as jnp
        import numpy as np
        B, S, H, E, K = (4, 256, 128, 8, 2)
        gates = jax.nn.softmax(x @ Wg + bg, axis=-1)
        top_k_gates, top_k_idx = jax.lax.top_k(gates, K)
        all_out = jnp.einsum('bsh,eho->bseo', x, W) + b
        sel = jnp.take_along_axis(all_out, top_k_idx[..., None], axis=2)
        out = jnp.sum(top_k_gates[..., None] * sel, axis=2)
        return out
    x = x + _L0_xattn_ref(ctx_768, _layernorm(x, axis=-1), mask_BxS2_bk0, L0_xattn_ln_x_g, L0_xattn_ln_x_b, L0_xattn_ln_l_g, L0_xattn_ln_l_b, L0_xattn_qn_g, L0_xattn_kn_g, L0_xattn_Wq, L0_xattn_Wkv, L0_xattn_Wlkv, L0_xattn_Wo, L0_xattn_bo)
    x = x + _L0_ffn_ref(_layernorm(x, axis=-1), L0_ffn_W, L0_ffn_b, L0_ffn_Wg, L0_ffn_bg)
    return x

_drawn_inputs = setup_inputs


def setup_inputs(seed=0):
    import zlib

    import numpy as np

    out = dict(_drawn_inputs(seed))
    spreads = {'L0_xattn_ln_x_g': (1.0, 0.6),
     'L0_xattn_ln_x_b': (0.0, 0.603),
     'L0_xattn_ln_l_g': (1.0, 0.2),
     'L0_xattn_ln_l_b': (0.0, 0.1),
     'L0_xattn_qn_g': (1.0, 0.2),
     'L0_xattn_kn_g': (1.0, 0.2),
     'L0_xattn_bo': (0.0, 0.1)}
    factors = {}
    for name, (base, spread) in spreads.items():
        noise = np.random.default_rng([zlib.crc32(name.encode()), seed]).standard_normal(out[name].shape)
        drawn = base * np.exp(spread * noise) if base else spread * noise
        out[name] = jnp.asarray(drawn.astype(out[name].dtype))
    for name, factor in factors.items():
        out[name] = (out[name] * factor).astype(out[name].dtype)
    return out
```

```python
from contextlib import ExitStack

import concourse.bass as bass
from concourse import mybir

ALU = mybir.AluOpType
ACT = mybir.ActivationFunctionType
AX = mybir.AxisListType
F32 = mybir.dt.float32
F32R = mybir.dt.float32r
U32 = mybir.dt.uint32
U8 = mybir.dt.uint8

P = 128
LN_EPS = 1e-5
RMS_EPS = 1e-8
MASKED = 1e30
SAFE_EXP = 60.0
RING = 3


def schedule(B, T, KT):
    steps = [("weights", 0, 0), ("ln1", 0, 0), ("params", 0, 0), ("xT", 0, 0)]
    steps += [("qkv", 0, t) for t in range(T)] + [("qknorm", 0, 0), ("kT", 0, 0), ("qT", 0, 0), ("constants", 0, 0)]
    for i in range(B + 1):
        now, nxt, old = i < B, i + 1 < B, i - 1 >= 0
        j = i - 1

        def score(n):
            return [("score", i, n)] if now else []

        def value(n):
            return [("value", i, n)] if now else []

        steps += score(0)
        if nxt:
            steps += [("ln1", i + 1, 0)]
        if old:
            steps += [("proj", j, t) for t in range(T)]
        if i == 0:
            steps += [("ctx_ln", 0, 0), ("ctxT", 0, 0)]
        if nxt:
            steps += [("xT", i + 1, 0)]
        if i == 0:
            steps += [("ctx_kv", 0, 0), ("ctx_kv", 0, 1)]
        steps += score(1) + value(0)
        if nxt:
            steps += [("qkv", i + 1, 0), ("qkv", i + 1, 1)]
        if i == 0:
            steps += [("ctx_norm", 0, 0), ("ctx_kT", 0, 0)]
        steps += score(2) + value(1)
        if old:
            steps += [("ln2", j, 0), ("l2T", j, 0)]
        if nxt:
            steps += [("qkv", i + 1, 2), ("qkv", i + 1, 3), ("qknorm", i + 1, 0)]
        steps += score(3) + value(2)
        if old:
            steps += [("gate", j, 0)]
        if nxt:
            steps += [("kT", i + 1, 0), ("qT", i + 1, 0)]
        steps += score(4) + value(3)
        if old:
            steps += [("experts_low", j, 0), ("gateT", j, 0), ("bias", j, 0), ("experts_high", j, 0)]
            steps += [("experts_low", j, 1), ("experts_high", j, 1)]
        steps += value(4)
        if now:
            steps += [("heads", i, 0)]
        if old:
            for t in (2, 3):
                steps += [("experts_low", j, t), ("experts_high", j, t)]
    return steps


def build(nc, x, ctx, mask, lxg, lxb, llg, llb, qng, kng, Wq, Wkv, Wlkv, Wo, bo, We, be, Wg, bg, out):
    B, S, C = x.shape
    _, M, CX = ctx.shape
    E = We.shape[0]
    D = qng.shape[0]
    H = C // D
    T = S // P
    KT = T + 1
    SCALE = float(D) ** -0.5
    EH = E // 2
    steps = schedule(B, T, KT)

    RING_JOBS = ("xT", "qkv", "kT", "qT", "ctxT", "ctx_kv", "ctx_kT", "proj", "l2T", "gate", "gateT", "bias",
                 "experts_low", "experts_high")
    jobs = [s for s in steps if s[0] in RING_JOBS]
    slot = {s: n % RING for n, s in enumerate(jobs)}
    before = {s: jobs[n - RING] for n, s in enumerate(jobs) if n >= RING}

    with ExitStack() as st:
        def sb(name, shape, dt=F32):
            return st.enter_context(nc.sbuf_tensor(name, shape, dt))

        def sem(name):
            return st.enter_context(nc.semaphore(name))

        x_sb = sb("x_sb", [P, B, T, C])
        xbo = sb("xbo", [P, T, C])
        ctx_sb = sb("ctx_sb", [M, B, CX])
        mask8 = sb("mask8", [B, M], U8)
        maskf = sb("maskf", [B, M])
        rows = sb("rows", [6, P])
        bo_b = sb("bo_b", [P, C])
        bg_b = sb("bg_b", [P, E])
        gq_b = sb("gq_b", [P, D])
        gk_b = sb("gk_b", [P, D])
        Wq_sb = sb("Wq_sb", [P, C])
        Wlkv_sb = sb("Wlkv_sb", [P, 2, C])
        Wkv_sb = sb("Wkv_sb", [P, 2, CX])
        Wo_sb = sb("Wo_sb", [P, C])
        We_sb = sb("We_sb", [P, E, C])
        WeH = sb("WeH", [P, E, C], F32R)
        WeL = sb("WeL", [P, E, C], F32R)
        WqkvH = sb("WqkvH", [P, 3 * C], F32R)
        WqkvL = sb("WqkvL", [P, 3 * C], F32R)
        WctxT = sb("WctxT", [CX, 2 * C])
        WoT = sb("WoT", [P, H, C])
        Wg_sb = sb("Wg_sb", [P, P])
        bias_blk = sb("bias_blk", [P, T, C])
        ident = sb("ident", [P, P])
        ones = sb("ones", [P, P])
        half = sb("half", [P, 16])
        iota_e = sb("iota_e", [P, E])
        cols = sb("cols", [P, 6])
        gain = sb("gain", [P, 1])
        gprod = sb("gprod", [P, D])
        gmax = sb("gmax", [P, 1])
        shift0 = sb("shift0", [P, 1])
        shift = sb("shift", [P, 1])
        mbias = sb("mbias", [M, B])
        cbias = sb("cbias", [M, B])
        cstat = sb("cstat", [M, B, 6])
        cmv = sb("cmv", [M, B, 2])
        cvar = sb("cvar", [M, B])
        crstd = sb("crstd", [M, B])
        cxh = sb("cxh", [M, B, CX])
        cT = sb("cT", [CX, B, M])
        ckv = sb("ckv", [P, B, 2 * C])
        csq = sb("csq", [M, B, C])
        css = sb("css", [M, B * H])
        cms = sb("cms", [M, B * H])
        crk = sb("crk", [M, B * H])
        ckn = sb("ckn", [M, B, C])
        cKH = sb("cKH", [P, B, M], F32R)
        cKL = sb("cKL", [P, B, M], F32R)
        stat1 = sb("stat1", [P, T, 6])
        mv1 = sb("mv1", [P, T, 2])
        var1 = sb("var1", [P, T])
        rstd1 = sb("rstd1", [P, T])
        xh = sb("xh", [P, T, C])
        lnT = sb("lnT", [P, S])
        lnH = sb("lnH", [P, S], F32R)
        lnL = sb("lnL", [P, S], F32R)
        qkv = [sb(f"qkv{n}", [P, T, 3 * C]) for n in range(2)]
        sq = sb("sq", [P, T, 2 * C])
        ss = sb("ss", [P, T * 2 * H])
        ms = sb("ms", [P, T * 2 * H])
        rqk = sb("rqk", [P, T * 2 * H])
        qkn = sb("qkn", [P, T, 2 * C])
        KH = [sb(f"KH{n}", [P, S], F32R) for n in range(2)]
        KL = [sb(f"KL{n}", [P, S], F32R) for n in range(2)]
        QH = [sb(f"QH{n}", [P, H, S], F32R) for n in range(2)]
        QL = [sb(f"QL{n}", [P, H, S], F32R) for n in range(2)]
        Es = [[sb(f"E{n}_{k}", [P, H, S]) for k in range(KT)] for n in range(2)]
        e01 = sb("e01", [P, H, S])
        esum = [sb(f"esum{n}", [P, H, S]) for n in range(2)]
        oT = sb("oT", [P, S])
        rden = sb("rden", [P, T, H])
        x2a = sb("x2a", [P, T, C])
        x2 = [sb(f"x2_{n}", [P, T, C]) for n in range(2)]
        x2b = [sb(f"x2b_{n}", [P, T, C]) for n in range(2)]
        stat2 = sb("stat2", [P, T, 6])
        mv2 = sb("mv2", [P, T, 2])
        var2 = sb("var2", [P, T])
        rstd2 = sb("rstd2", [P, T])
        l2 = sb("l2", [P, T, C])
        l2T = sb("l2T", [P, S])
        l2H = sb("l2H", [P, S], F32R)
        l2L = sb("l2L", [P, S], F32R)
        lg = sb("lg", [P, T, E])
        nmx = sb("nmx", [P, T])
        lgs = sb("lgs", [P, T, E])
        eg = sb("eg", [P, T, E])
        esm = sb("esm", [P, T])
        erc = sb("erc", [P, T])
        top = sb("top", [P, T, 8])
        topi = sb("topi", [P, T, 8], U32)
        topf = sb("topf", [P, T, 2])
        eq1 = sb("eq1", [P, T, E])
        eq2 = sb("eq2", [P, T, E])
        er = sb("er", [P, T, E])
        w = [sb(f"w{n}", [P, T, E]) for n in range(2)]
        wT = sb("wT", [P, P])
        scaled = [sb(f"scaled{n}", [P, EH, C]) for n in range(2)]
        pair = sb("pair", [P, EH // 2, C])
        low = sb("low", [P, C])
        acc = [sb(f"acc{n}", [P, C]) for n in range(2)]
        part = [sb(f"part{n}", [P, C]) for n in range(3)]
        res = [sb(f"res{n}", [P, T, C]) for n in range(2)]

        S_ps = [st.enter_context(nc.psum_tensor(f"S_ps{n}", [P, H, S], F32)) for n in range(2)]
        O_ps = st.enter_context(nc.psum_tensor("O_ps", [P, S], F32))
        R_ps = [st.enter_context(nc.psum_tensor(f"R_ps{n}", [P, S], F32)) for n in range(RING)]

        def ring(kind, i, t):
            return R_ps[slot[(kind, i, t)]]

        x_in = [sem(f"x_in{n}") for n in range(B)]
        Wlat_in, Wout_in, Wctx_in, We_in, Wg_in = sem("Wlat_in"), sem("Wout_in"), sem("Wctx_in"), sem("We_in"), sem("Wg_in")
        rows_in, bcast_in, ctx_in, blk_in = sem("rows_in"), sem("bcast_in"), sem("ctx_in"), sem("blk_in")
        stored = [sem(f"stored{n}") for n in range(B)]
        ident_made, half_made, rows_zeroed, zeroed, ones_made, iota_made = (
            sem("ident_made"), sem("half_made"), sem("rows_zeroed"), sem("zeroed"), sem("ones_made"), sem("iota_made"))
        Wg_zeroed, blk_zeroed = sem("Wg_zeroed"), sem("blk_zeroed")
        mask_made, cols_ps, cols_made, gain_made, shift_made, cbias_made = (
            sem("mask_made"), sem("cols_ps"), sem("cols_made"), sem("gain_made"), sem("shift_made"), sem("cbias_made"))
        Wlat_ps, Wout_ps, Wctx_ps = sem("Wlat_ps"), sem("Wout_ps"), sem("Wctx_ps")
        WqkvH_made, WqkvL_made, WoT_made, WctxT_made = sem("WqkvH_made"), sem("WqkvL_made"), sem("WoT_made"), sem("WctxT_made")
        WeH_made, WeL_made = sem("WeH_made"), sem("WeL_made")
        cmv_made, crstd_made, cxh_made, ctxT_ps, cT_made = (
            sem("cmv_made"), sem("crstd_made"), sem("cxh_made"), sem("ctxT_ps"), sem("cT_made"))
        ckv_ps, ckv_made, css_made, crk_made, ckn_made, ckT_ps, cKH_made, cKL_made = (
            sem("ckv_ps"), sem("ckv_made"), sem("css_made"), sem("crk_made"), sem("ckn_made"), sem("ckT_ps"),
            sem("cKH_made"), sem("cKL_made"))
        mv1_made, rstd1_made, xh_made, xT_ps, lnT_made, lnH_made, lnL_made = (
            sem("mv1_made"), sem("rstd1_made"), sem("xh_made"), sem("xT_ps"), sem("lnT_made"), sem("lnH_made"), sem("lnL_made"))
        qkv_ps, qkv_made, sq_made, ss_made, rqk_made, qkn_made = (
            sem("qkv_ps"), sem("qkv_made"), sem("sq_made"), sem("ss_made"), sem("rqk_made"), sem("qkn_made"))
        kT_ps, KH_made, KL_made, qT_ps, QH_made, QL_made = (
            sem("kT_ps"), sem("KH_made"), sem("KL_made"), sem("qT_ps"), sem("QH_made"), sem("QL_made"))
        scores_ps, probs_made, O_done, oT_made, e01_made, esum_made = (
            sem("scores_ps"), sem("probs_made"), sem("O_done"), sem("oT_made"), sem("e01_made"), sem("esum_made"))
        xbo_made, proj_ps, x2_made, mv2_made, rstd2_made, l2_made, l2T_ps, l2T_made, l2H_made, l2L_made = (
            sem("xbo_made"), sem("proj_ps"), sem("x2_made"), sem("mv2_made"), sem("rstd2_made"), sem("l2_made"),
            sem("l2T_ps"), sem("l2T_made"), sem("l2H_made"), sem("l2L_made"))
        gate_ps, lg_made, lgs_made, eg_made, w_made, gateT_ps, wT_made, bias_ps, x2b_made = (
            sem("gate_ps"), sem("lg_made"), sem("lgs_made"), sem("eg_made"), sem("w_made"), sem("gateT_ps"),
            sem("wT_made"), sem("bias_ps"), sem("x2b_made"))
        low_ps, high_ps, scaled_made, acc_made, res_made = (
            sem("low_ps"), sem("high_ps"), sem("scaled_made"), sem("acc_made"), sem("res_made"))
        dve_step, act_step, pool_step = sem("dve_step"), sem("act_step"), sem("pool_step")

        RELEASED = {
            "xT": lambda i, t: (lnT_made, i + 1),
            "qkv": lambda i, t: (qkv_made, T * i + t + 1),
            "kT": lambda i, t: (KL_made, i + 1),
            "qT": lambda i, t: (QL_made, i + 1),
            "ctxT": lambda i, t: (cT_made, 1),
            "ctx_kv": lambda i, t: (ckv_made, t + 1),
            "ctx_kT": lambda i, t: (cKL_made, 1),
            "proj": lambda i, t: (x2_made, T * i + t + 1),
            "l2T": lambda i, t: (l2T_made, i + 1),
            "gate": lambda i, t: (lg_made, i + 1),
            "gateT": lambda i, t: (wT_made, i + 1),
            "bias": lambda i, t: (x2b_made, i + 1),
            "experts_low": lambda i, t: (scaled_made, T * i + t + 1),
            "experts_high": lambda i, t: (acc_made, T * i + t + 1),
        }

        def row(v):
            return v.rearrange("(a d) -> a d", a=1)

        block = st.enter_context(nc.Block())

        @block.sync
        def _(sp):
            sp.dma_start(x_sb[:, 0], x[0].rearrange("(p t) c -> p t c", t=T)).then_inc(x_in[0], 16)
            sp.dma_start(Wq_sb[:], Wq).then_inc(Wlat_in, 16)
            sp.dma_start(Wlkv_sb[:], Wlkv.rearrange("(a o) c -> o a c", a=2)).then_inc(Wlat_in, 16)
            sp.wait_ge(rows_zeroed, 1)
            for n, v in enumerate((llg, llb)):
                sp.dma_start(rows[n:n + 1, :], row(v)).then_inc(rows_in, 16)
            for n, v in enumerate((qng, kng)):
                for h in range(H):
                    sp.dma_start(rows[2 + n:3 + n, h * D:(h + 1) * D], row(v)).then_inc(rows_in, 16)
            for n, v in enumerate((lxg, lxb)):
                sp.dma_start(rows[4 + n:5 + n, 0:CX], row(v)).then_inc(rows_in, 16)
            sp.dma_start(mask8[:], mask).then_inc(rows_in, 16)
            sp.dma_start(ctx_sb[:], ctx.rearrange("b m c -> m b c")).then_inc(ctx_in, 16)
            for i in range(1, B):
                sp.dma_start(x_sb[:, i], x[i].rearrange("(p t) c -> p t c", t=T)).then_inc(x_in[i], 16)
            for i in range(B):
                dst = out[i].rearrange("(p t) c -> p t c", t=T)
                if i < B - 1:
                    sp.wait_ge(res_made, T * (i + 1))
                    sp.dma_start(dst, res[i % 2][:]).then_inc(stored[i], 16)
                else:
                    for t in range(T):
                        sp.wait_ge(res_made, T * i + t + 1)
                        sp.dma_start(dst[:, t], res[i % 2][:, t]).then_inc(stored[i], 16)
            for i in range(B):
                sp.wait_ge(stored[i], 16 * (T if i == B - 1 else 1))

        @block.gpsimd
        def _(pool):
            count = [0]

            def step(ins):
                count[0] += 1
                ins.then_inc(pool_step, 1)
                pool.wait_ge(pool_step, count[0])

            def power_half(dst, ready):
                pass

            step(pool.memset(ident[:], 0.0))
            pool.affine_select(out=ident[:], in_=ident[:], compare_op=ALU.not_equal, fill=1.0, base=0,
                               pattern=[[-1, P]], channel_multiplier=1).then_inc(ident_made, 1)
            pool.memset(half[:], -0.5).then_inc(half_made, 1)

            def constants():
                pool.memset(Wg_sb[:], 0.0).then_inc(Wg_zeroed, 1)
                pool.wait_ge(Wg_zeroed, 1)
                pool.dma_start(Wg_sb[:, 0:E], Wg).then_inc(Wg_in, 16)
                pool.memset(bias_blk[:], 0.0).then_inc(blk_zeroed, 1)
                pool.wait_ge(blk_zeroed, 1)
                for t in range(T):
                    pool.dma_start(bias_blk[E * t:E * (t + 1), t], be).then_inc(blk_in, 16)
                pool.iota(iota_e[:], pattern=[[1, E]], base=0, channel_multiplier=0,
                          allow_small_or_imprecise_dtypes=True).then_inc(iota_made, 1)

            def ln1(i):
                pool.wait_ge(mv1_made, i + 1)
                pool.wait_ge(half_made, 1)
                step(pool.tensor_scalar(var1[:], mv1[:, :, 1], 1.0 + LN_EPS, LN_EPS * LN_EPS, ALU.mult, ALU.add))
                pool.tensor_tensor(rstd1[:], var1[:], half[:, 0:T], ALU.pow).then_inc(rstd1_made, 1)

            def xT(i):
                pool.wait_ge(lnH_made, i + 1)
                pool.tensor_tensor(lnL[:], lnT[:], lnH[:].bitcast(F32), ALU.subtract).then_inc(lnL_made, 1)

            def qknorm(i):
                pool.wait_ge(ss_made, i + 1)
                step(pool.tensor_scalar(ms[:], ss[:], 1.0 / D, RMS_EPS * RMS_EPS, ALU.mult, ALU.max))
                pool.tensor_tensor(rqk[:], ms[:], half[:], ALU.pow).then_inc(rqk_made, 1)

            def ctx_ln():
                pool.wait_ge(cmv_made, 1)
                step(pool.tensor_scalar(cvar[:], cmv[:, :, 1], 1.0, LN_EPS, ALU.mult, ALU.add))
                pool.tensor_tensor(crstd[:], cvar[:], half[0:M, 0:B], ALU.pow).then_inc(crstd_made, 1)

            def ctx_norm():
                pool.wait_ge(css_made, 1)
                step(pool.tensor_scalar(cms[:], css[:], 1.0 / D, RMS_EPS * RMS_EPS, ALU.mult, ALU.max))
                pool.tensor_tensor(crk[:], cms[:], half[0:M, 0:B * H], ALU.pow).then_inc(crk_made, 1)

            def value(i, n):
                if n == 1:
                    pool.wait_ge(probs_made, KT * i + 2)
                    if i >= 1:
                        pool.wait_ge(esum_made, i)
                    pool.tensor_tensor(e01[:], Es[i % 2][0][:], Es[i % 2][1][:], ALU.add).then_inc(e01_made, 1)
                if n == 2:
                    pool.wait_ge(bcast_in, 16 * 4)
                    if i >= 1:
                        pool.wait_ge(x2_made, T * i)
                    pool.tensor_tensor(xbo[:], x_sb[:, i], bo_b[:].unsqueeze(1).to_broadcast([P, T, C]),
                                       ALU.add).then_inc(xbo_made, 1)

            def ln2(i):
                pool.wait_ge(mv2_made, i + 1)
                step(pool.tensor_scalar(var2[:], mv2[:, :, 1], 1.0, LN_EPS, ALU.mult, ALU.add))
                pool.tensor_tensor(rstd2[:], var2[:], half[:, 0:T], ALU.pow).then_inc(rstd2_made, 1)

            def l2T_(i):
                pool.wait_ge(l2H_made, i + 1)
                pool.tensor_tensor(l2L[:], l2T[:], l2H[:].bitcast(F32), ALU.subtract).then_inc(l2L_made, 1)

            def experts(i, t):
                n = T * i + t
                pool.wait_ge(scaled_made, n + 1)
                step(pool.tensor_tensor(pair[:], scaled[n % 2][:, 0:EH // 2], scaled[n % 2][:, EH // 2:EH], ALU.add))
                step(pool.tensor_tensor(low[:], pair[:, 0], pair[:, 1], ALU.add))
                pool.wait_ge(acc_made, n + 1)
                if t == 0 and i >= 2:
                    pool.wait_ge(stored[i - 2], 16)
                pool.tensor_tensor(res[i % 2][:, t], low[:], acc[n % 2][:], ALU.add).then_inc(res_made, 1)

            for kind, i, t in steps:
                if kind == "constants":
                    constants()
                elif kind == "ln1":
                    ln1(i)
                elif kind == "xT":
                    xT(i)
                elif kind == "qknorm":
                    qknorm(i)
                elif kind == "ctx_ln":
                    ctx_ln()
                elif kind == "ctx_norm":
                    ctx_norm()
                elif kind == "value":
                    value(i, t)
                elif kind == "ln2":
                    ln2(i)
                elif kind == "l2T":
                    l2T_(i)
                elif kind == "experts_high":
                    experts(i, t)

        @block.scalar
        def _(act):
            act.dma_start(Wo_sb[:], Wo).then_inc(Wout_in, 16)
            act.dma_start(Wkv_sb[:], Wkv.rearrange("(a o) c -> o a c", a=2)).then_inc(Wctx_in, 16)
            act.dma_start(bo_b[:], row(bo).to_broadcast([P, C])).then_inc(bcast_in, 16)
            act.dma_start(bg_b[:], row(bg).to_broadcast([P, E])).then_inc(bcast_in, 16)
            act.dma_start(gq_b[:], row(qng).to_broadcast([P, D])).then_inc(bcast_in, 16)
            act.dma_start(gk_b[:], row(kng).to_broadcast([P, D])).then_inc(bcast_in, 16)
            act.dma_start(We_sb[:], We.rearrange("e h o -> h e o")).then_inc(We_in, 16)

            def weights():
                act.wait_ge(Wlat_ps, 1)
                act.copy(WqkvH[:], S_ps[0][:, 0, 0:3 * C]).then_inc(WqkvH_made, 1)

            def xT(i):
                act.wait_ge(xT_ps, i + 1)
                act.wait_ge(cols_made, 1)
                act.activation(lnT[:], ring("xT", i, 0)[:], ACT.Identity, bias=cols[:, 1:2],
                               scale=cols[:, 0:1]).then_inc(lnT_made, 1)

            def qkv_copy(i, t):
                act.wait_ge(qkv_ps, T * i + t + 1)
                act.copy(qkv[i % 2][:, t], ring("qkv", i, t)[:, 0:3 * C]).then_inc(qkv_made, 1)

            def qknorm(i):
                act.wait_ge(qkv_made, T * (i + 1))
                act.activation(sq[:], qkv[i % 2][:, :, 0:2 * C], ACT.Square).then_inc(sq_made, 1)

            def kT(i):
                act.wait_ge(kT_ps, i + 1)
                act.wait_ge(gain_made, 1)
                act.activation(KH[i % 2][:], ring("kT", i, 0)[:], ACT.Identity,
                               scale=gain[:, 0:1]).then_inc(KH_made, 1)

            def qT(i):
                act.wait_ge(qT_ps, i + 1)
                for h in range(H):
                    r = slice(h * D, (h + 1) * D)
                    act.copy(QH[i % 2][r, h], ring("qT", i, 0)[r, :]).then_inc(QH_made, 1)

            def constants():
                act.wait_ge(Wout_ps, 1)
                act.wait_ge(zeroed, 1)
                for h in range(H):
                    r = slice(h * D, (h + 1) * D)
                    act.copy(WoT[r, h], S_ps[1][r, 0, 0:C]).then_inc(WoT_made, 1)
                act.wait_ge(Wctx_ps, 1)
                act.copy(WctxT[:], S_ps[1][0:CX, 1, 0:2 * C]).then_inc(WctxT_made, 1)

            def ctxT():
                act.wait_ge(ctxT_ps, 1)
                act.activation(cT[:].rearrange("c b m -> c (b m)"), ring("ctxT", 0, 0)[0:CX, 0:B * M], ACT.Identity,
                               bias=cols[0:CX, 5:6], scale=cols[0:CX, 4:5]).then_inc(cT_made, 1)

            def ctx_kv(n):
                act.wait_ge(ckv_ps, n + 1)
                act.wait_ge(zeroed, 1)
                act.copy(ckv[0:M, 2 * n:2 * n + 2].rearrange("m b c -> m (b c)"),
                         ring("ctx_kv", 0, n)[0:M, :]).then_inc(ckv_made, 1)

            def ctx_kT():
                act.wait_ge(ckT_ps, 1)
                act.activation(cKH[:].rearrange("c b m -> c (b m)"), ring("ctx_kT", 0, 0)[:, 0:B * M], ACT.Identity,
                               scale=gain[:, 0:1]).then_inc(cKH_made, 1)

            def score(i, n):
                g = KT * i + n
                act.wait_ge(scores_ps, g + 1)
                if g == 0:
                    act.wait_ge(shift_made, 1)
                    act.wait_ge(zeroed, 1)
                if i >= 2 and n == 0:
                    act.wait_ge(O_done, i - 1)
                    act.wait_ge(esum_made, i - 1)
                if n < T:
                    act.activation(Es[i % 2][n][:], S_ps[g % 2][:], ACT.Exp, bias=shift[:, 0:1]).then_inc(probs_made, 1)
                else:
                    if i == 0:
                        act.wait_ge(cbias_made, 1)
                    act.activation(Es[i % 2][n][0:M], S_ps[g % 2][0:M], ACT.Exp,
                                   bias=cbias[:, i:i + 1]).then_inc(probs_made, 1)

            def heads(i):
                act.wait_ge(O_done, i + 1)
                act.copy(oT[:], O_ps[:]).then_inc(oT_made, 1)

            def l2T_(i):
                act.wait_ge(l2T_ps, i + 1)
                if i >= 1:
                    act.wait_ge(l2L_made, i)
                act.copy(l2T[:], ring("l2T", i, 0)[:]).then_inc(l2T_made, 1)

            def gate(i):
                act.wait_ge(lgs_made, i + 1)
                act.activation(eg[:], lgs[:], ACT.Exp).then_inc(eg_made, 1)

            def experts_low(i, t):
                n = T * i + t
                act.wait_ge(low_ps, n + 1)
                act.wait_ge(w_made, i + 1)
                if n >= 2:
                    act.wait_ge(res_made, n - 1)
                ps = ring("experts_low", i, t)[:].rearrange("p (e c) -> p e c", e=EH)
                for e in range(EH):
                    last = act.activation(scaled[n % 2][:, e], ps[:, e], ACT.Copy, scale=w[i % 2][:, t, e:e + 1])
                last.then_inc(scaled_made, 1)

            for kind, i, t in steps:
                if kind == "weights":
                    weights()
                elif kind == "xT":
                    xT(i)
                elif kind == "qkv":
                    qkv_copy(i, t)
                elif kind == "qknorm":
                    qknorm(i)
                elif kind == "kT":
                    kT(i)
                elif kind == "qT":
                    qT(i)
                elif kind == "constants":
                    constants()
                elif kind == "ctxT":
                    ctxT()
                elif kind == "ctx_kv":
                    ctx_kv(t)
                elif kind == "ctx_kT":
                    ctx_kT()
                elif kind == "score":
                    score(i, t)
                elif kind == "heads":
                    heads(i)
                elif kind == "l2T":
                    l2T_(i)
                elif kind == "gate":
                    gate(i)
                elif kind == "experts_low":
                    experts_low(i, t)

        @block.vector
        def _(dve):
            count = [0]

            def step(ins):
                count[0] += 1
                ins.then_inc(dve_step, 1)
                return count[0]

            def weights():
                dve.memset(rows[:], 0.0).then_inc(rows_zeroed, 1)
                for n in range(2):
                    dve.memset(QH[n][:].bitcast(F32), 0.0)
                    dve.memset(QL[n][:].bitcast(F32), 0.0)
                dve.memset(ones[:], 1.0).then_inc(ones_made, 1)

            def params():
                dve.wait_ge(rows_in, 16 * 9)
                dve.tensor_copy(maskf[:], mask8[:]).then_inc(mask_made, 1)
                dve.wait_ge(cols_ps, 1)
                dve.tensor_copy(cols[:], S_ps[0][:, 1, 0:6]).then_inc(cols_made, 1)
                dve.wait_ge(cols_made, 1)
                dve.scalar_tensor_tensor(gain[:], cols[:, 2:3], SCALE, cols[:, 3:4], ALU.mult,
                                         ALU.mult).then_inc(gain_made, 1)

            def bounds():
                dve.wait_ge(bcast_in, 16 * 4)
                n = step(dve.tensor_tensor(gprod[:], gq_b[:], gk_b[:], ALU.mult))
                dve.wait_ge(dve_step, n)
                n = step(dve.tensor_reduce(gmax[:], gprod[:], AX.X, ALU.max, apply_absolute_value=True))
                dve.wait_ge(dve_step, n)
                n = step(dve.tensor_scalar(shift0[:], gmax[:], -D * SCALE, SAFE_EXP, ALU.mult, ALU.add))
                dve.wait_ge(dve_step, n)
                dve.tensor_scalar(shift[:], shift0[:], 0.0, None, ALU.min).then_inc(shift_made, 1)
                n = step(dve.tensor_scalar(mbias[:], S_ps[0][0:M, 1, 8:8 + B], 1.0, MASKED, ALU.subtract, ALU.mult))
                dve.wait_ge(dve_step, n)
                dve.wait_ge(shift_made, 1)
                dve.tensor_scalar(cbias[:], mbias[:], shift[0:M, 0:1], None, ALU.add).then_inc(cbias_made, 1)

            def weights_low():
                dve.wait_ge(WqkvH_made, 1)
                dve.tensor_tensor(WqkvL[:], S_ps[0][:, 0, 0:3 * C], WqkvH[:].bitcast(F32),
                                  ALU.subtract).then_inc(WqkvL_made, 1)

            def constants():
                dve.memset(WoT[:], 0.0)
                dve.memset(ckv[:], 0.0)
                dve.memset(wT[:], 0.0)
                for n in range(2):
                    last = dve.memset(Es[n][T][:], 0.0)
                last.then_inc(zeroed, 1)
                bounds()

            def experts_split():
                dve.wait_ge(We_in, 16)
                dve.tensor_copy(WeH[:], We_sb[:]).then_inc(WeH_made, 1)
                dve.wait_ge(WeH_made, 1)
                dve.tensor_tensor(WeL[:], We_sb[:], WeH[:].bitcast(F32), ALU.subtract).then_inc(WeL_made, 1)

            def ln1(i):
                dve.wait_ge(x_in[i], 16)
                for t in range(T):
                    last = dve.bn_stats(stat1[:, t], x_sb[:, i, t])
                dve.wait_ge(dve_step, step(last))
                for t in range(T):
                    last = dve.bn_aggr(mv1[:, t], stat1[:, t])
                last.then_inc(mv1_made, 1)

            def ln1_apply(i):
                dve.wait_ge(rstd1_made, i + 1)
                for t in range(T):
                    last = dve.tensor_scalar(xh[:, t], x_sb[:, i, t], mv1[:, t, 0:1], rstd1[:, t:t + 1],
                                             ALU.subtract, ALU.mult)
                last.then_inc(xh_made, 1)

            def ln_high(i):
                dve.wait_ge(lnT_made, i + 1)
                dve.tensor_copy(lnH[:], lnT[:]).then_inc(lnH_made, 1)

            def qknorm(i):
                dve.wait_ge(sq_made, i + 1)
                dve.tensor_reduce(ss[:], sq[:].rearrange("p t (g d) -> p (t g) d", d=D), AX.X,
                                  ALU.add).then_inc(ss_made, 1)
                dve.wait_ge(rqk_made, i + 1)
                dve.tensor_tensor(qkn[:].rearrange("p t (g d) -> p t g d", d=D),
                                  qkv[i % 2][:, :, 0:2 * C].rearrange("p t (g d) -> p t g d", d=D),
                                  rqk[:].rearrange("p (t g) -> p t g", t=T).unsqueeze(3).to_broadcast([P, T, 2 * H, D]),
                                  ALU.mult).then_inc(qkn_made, 1)

            def kT(i):
                dve.wait_ge(KH_made, i + 1)
                dve.scalar_tensor_tensor(KL[i % 2][:], ring("kT", i, 0)[:], gain[:, 0:1], KH[i % 2][:].bitcast(F32),
                                         ALU.mult, ALU.subtract).then_inc(KL_made, 1)

            def qT(i):
                dve.wait_ge(QH_made, H * (i + 1))
                for h in range(H):
                    r = slice(h * D, (h + 1) * D)
                    last = dve.tensor_tensor(QL[i % 2][r, h], ring("qT", i, 0)[r, :], QH[i % 2][r, h].bitcast(F32),
                                             ALU.subtract)
                last.then_inc(QL_made, 1)

            def ctx_ln():
                dve.wait_ge(ctx_in, 16)
                for b in range(B):
                    last = dve.bn_stats(cstat[:, b], ctx_sb[:, b])
                dve.wait_ge(dve_step, step(last))
                for b in range(B):
                    last = dve.bn_aggr(cmv[:, b], cstat[:, b])
                last.then_inc(cmv_made, 1)
                dve.wait_ge(crstd_made, 1)
                for b in range(B):
                    last = dve.tensor_scalar(cxh[:, b], ctx_sb[:, b], cmv[:, b, 0:1], crstd[:, b:b + 1],
                                             ALU.subtract, ALU.mult)
                last.then_inc(cxh_made, 1)

            def ctx_norm():
                dve.wait_ge(ckv_made, 2)
                dve.wait_ge(dve_step, step(dve.tensor_tensor(csq[:], ckv[0:M, :, 0:C], ckv[0:M, :, 0:C], ALU.mult)))
                dve.tensor_reduce(css[:], csq[:].rearrange("m b (h d) -> m (b h) d", d=D), AX.X,
                                  ALU.add).then_inc(css_made, 1)
                dve.wait_ge(crk_made, 1)
                dve.tensor_tensor(ckn[:].rearrange("m b (h d) -> m b h d", d=D),
                                  ckv[0:M, :, 0:C].rearrange("m b (h d) -> m b h d", d=D),
                                  crk[:].rearrange("m (b h) -> m b h", b=B).unsqueeze(3).to_broadcast([M, B, H, D]),
                                  ALU.mult).then_inc(ckn_made, 1)

            def ctx_kT():
                dve.wait_ge(cKH_made, 1)
                dve.scalar_tensor_tensor(cKL[:].rearrange("c b m -> c (b m)"), ring("ctx_kT", 0, 0)[:, 0:B * M],
                                         gain[:, 0:1], cKH[:].rearrange("c b m -> c (b m)").bitcast(F32),
                                         ALU.mult, ALU.subtract).then_inc(cKL_made, 1)

            def value(i, n):
                E_ = Es[i % 2]
                if n == 3:
                    dve.wait_ge(probs_made, KT * i + 4)
                    if i >= 2:
                        dve.wait_ge(proj_ps, T * (i - 1))
                    step(dve.tensor_tensor(esum[i % 2][:], E_[2][:], E_[3][:], ALU.add))
                if n == 4:
                    dve.wait_ge(dve_step, count[0])
                    dve.wait_ge(e01_made, i + 1)
                    step(dve.tensor_tensor(esum[i % 2][:], esum[i % 2][:], e01[:], ALU.add))
                    dve.wait_ge(dve_step, count[0])
                    dve.wait_ge(probs_made, KT * (i + 1))
                    dve.tensor_tensor(esum[i % 2][0:M], esum[i % 2][0:M], E_[4][0:M], ALU.add).then_inc(esum_made, 1)

            def proj(i, t):
                dve.wait_ge(proj_ps, T * i + t + 1)
                dve.wait_ge(xbo_made, i + 1)
                ps = ring("proj", i, t)[:].rearrange("p (g c) -> p g c", c=C)
                dve.wait_ge(dve_step, step(dve.reciprocal(rden[:, t], ps[:, H:2 * H, 0])))
                dve.wait_ge(dve_step, step(dve.scalar_tensor_tensor(
                    x2a[:, t], ps[:, 0], rden[:, t, 0:1], xbo[:, t], ALU.mult, ALU.add)))
                dve.scalar_tensor_tensor(x2[i % 2][:, t], ps[:, 1], rden[:, t, 1:2], x2a[:, t],
                                         ALU.mult, ALU.add).then_inc(x2_made, 1)

            def ln2(i):
                dve.wait_ge(x2_made, T * (i + 1))
                for t in range(T):
                    last = dve.bn_stats(stat2[:, t], x2[i % 2][:, t])
                dve.wait_ge(dve_step, step(last))
                for t in range(T):
                    last = dve.bn_aggr(mv2[:, t], stat2[:, t])
                last.then_inc(mv2_made, 1)
                dve.wait_ge(rstd2_made, i + 1)
                for t in range(T):
                    last = dve.tensor_scalar(l2[:, t], x2[i % 2][:, t], mv2[:, t, 0:1], rstd2[:, t:t + 1],
                                             ALU.subtract, ALU.mult)
                last.then_inc(l2_made, 1)

            def l2T_(i):
                dve.wait_ge(l2T_made, i + 1)
                dve.tensor_copy(l2H[:], l2T[:]).then_inc(l2H_made, 1)

            def gate(i):
                dve.wait_ge(gate_ps, i + 1)
                dve.wait_ge(iota_made, 1)
                dve.tensor_tensor(lg[:], ring("gate", i, 0)[:].rearrange("p (t c) -> p t c", t=T)[:, :, 0:E],
                                  bg_b[:].unsqueeze(1).to_broadcast([P, T, E]), ALU.add).then_inc(lg_made, 1)
                dve.wait_ge(lg_made, i + 1)
                dve.wait_ge(dve_step, step(dve.tensor_reduce(nmx[:], lg[:], AX.X, ALU.max, negate=True)))
                dve.tensor_tensor(lgs[:], lg[:], nmx[:].unsqueeze(2).to_broadcast([P, T, E]),
                                  ALU.add).then_inc(lgs_made, 1)
                dve.wait_ge(eg_made, i + 1)
                for t in range(T):
                    last = dve.max(top[:, t], eg[:, t])
                maxed = step(last)
                summed = step(dve.tensor_reduce(esm[:], eg[:], AX.X, ALU.add))
                dve.wait_ge(dve_step, maxed)
                for t in range(T):
                    last = dve.max_index(topi[:, t], top[:, t], eg[:, t])
                indexed = step(last)
                dve.wait_ge(dve_step, summed)
                inverse = step(dve.reciprocal(erc[:], esm[:]))
                dve.wait_ge(dve_step, indexed)
                numbers = step(dve.tensor_copy(topf[:], topi[:, :, 0:2]))
                dve.wait_ge(dve_step, inverse)
                step(dve.tensor_tensor(er[:], eg[:], erc[:].unsqueeze(2).to_broadcast([P, T, E]), ALU.mult))
                dve.wait_ge(dve_step, numbers)
                every = iota_e[:].unsqueeze(1).to_broadcast([P, T, E])
                step(dve.tensor_tensor(eq1[:], every, topf[:, :, 0:1].to_broadcast([P, T, E]), ALU.is_equal))
                step(dve.tensor_tensor(eq2[:], every, topf[:, :, 1:2].to_broadcast([P, T, E]), ALU.is_equal))
                dve.wait_ge(dve_step, count[0])
                dve.wait_ge(dve_step, step(dve.tensor_tensor(eq1[:], eq1[:], eq2[:], ALU.add)))
                if i >= 2:
                    dve.wait_ge(scaled_made, T * (i - 1))
                dve.tensor_tensor(w[i % 2][:], er[:], eq1[:], ALU.mult).then_inc(w_made, 1)

            def gateT(i):
                dve.wait_ge(gateT_ps, i + 1)
                dve.tensor_copy(wT[0:T * E], ring("gateT", i, 0)[0:T * E, 0:P]).then_inc(wT_made, 1)

            def bias(i):
                dve.wait_ge(bias_ps, i + 1)
                dve.tensor_tensor(x2b[i % 2][:].rearrange("p t c -> p (t c)"), ring("bias", i, 0)[:],
                                  x2[i % 2][:].rearrange("p t c -> p (t c)"), ALU.add).then_inc(x2b_made, 1)
                dve.wait_ge(x2b_made, i + 1)

            def experts_high(i, t):
                n = T * i + t
                dve.wait_ge(high_ps, n + 1)
                ps = ring("experts_high", i, t)[:].rearrange("p (e c) -> p e c", e=EH)
                src = x2b[i % 2][:, t]
                if n >= 2:
                    dve.wait_ge(res_made, n - 1)
                for e in range(EH):
                    last = e == EH - 1
                    dst = acc[n % 2][:] if last else part[e][:]
                    ins = dve.scalar_tensor_tensor(dst, ps[:, e], w[i % 2][:, t, EH + e:EH + e + 1], src,
                                                   ALU.mult, ALU.add)
                    if last:
                        ins.then_inc(acc_made, 1)
                    else:
                        dve.wait_ge(dve_step, step(ins))
                    src = dst

            for kind, i, t in steps:
                if kind == "weights":
                    weights()
                elif kind == "params":
                    params()
                    weights_low()
                elif kind == "constants":
                    constants()
                elif kind == "ln1":
                    ln1(i)
                    ln1_apply(i)
                elif kind == "xT":
                    if i == 1:
                        experts_split()
                    ln_high(i)
                elif kind == "qknorm":
                    qknorm(i)
                elif kind == "kT":
                    kT(i)
                elif kind == "qT":
                    qT(i)
                elif kind == "ctx_ln":
                    ctx_ln()
                elif kind == "ctx_norm":
                    ctx_norm()
                elif kind == "ctx_kT":
                    ctx_kT()
                elif kind == "value":
                    value(i, t)
                elif kind == "proj":
                    proj(i, t)
                elif kind == "ln2":
                    ln2(i)
                elif kind == "l2T":
                    l2T_(i)
                elif kind == "gate":
                    gate(i)
                elif kind == "gateT":
                    gateT(i)
                elif kind == "bias":
                    bias(i)
                elif kind == "experts_high":
                    experts_high(i, t)

        @block.tensor
        def _(pe):
            def free(kind, i, t):
                if (kind, i, t) in before:
                    k, bi, bt = before[(kind, i, t)]
                    pe.wait_ge(*RELEASED[k](bi, bt))

            def three(dst, lH, lL, rH, rL):
                pe.matmul(dst, lH, rH, start=True, stop=False)
                pe.matmul(dst, lH, rL, start=False, stop=False)
                return pe.matmul(dst, lL, rH, start=False, stop=True)

            def weights():
                pe.wait_ge(ident_made, 1)
                pe.wait_ge(Wlat_in, 32)
                pe.transpose(S_ps[0][:, 0, 0:C], Wq_sb[:], ident[:])
                for a in range(2):
                    last = pe.transpose(S_ps[0][:, 0, (a + 1) * C:(a + 2) * C], Wlkv_sb[:, a], ident[:])
                last.then_inc(Wlat_ps, 1)

            def params():
                pe.wait_ge(rows_in, 16 * 9)
                pe.wait_ge(mask_made, 1)
                pe.transpose(S_ps[0][:, 1, 0:6], rows[:], ident[0:6, 0:6])
                pe.transpose(S_ps[0][0:M, 1, 8:8 + B], maskf[:], ident[0:B, 0:B]).then_inc(cols_ps, 1)

            def constants():
                pe.wait_ge(Wout_in, 16)
                pe.transpose(S_ps[1][:, 0, 0:C], Wo_sb[:], ident[:]).then_inc(Wout_ps, 1)
                pe.wait_ge(Wctx_in, 16)
                for a in range(2):
                    last = pe.transpose(S_ps[1][0:CX, 1, a * C:(a + 1) * C], Wkv_sb[:, a], ident[:])
                last.then_inc(Wctx_ps, 1)

            def xT(i):
                free("xT", i, 0)
                pe.wait_ge(xh_made, i + 1)
                for t in range(T):
                    last = pe.transpose(ring("xT", i, 0)[:, t * P:(t + 1) * P], xh[:, t], ident[:])
                last.then_inc(xT_ps, 1)

            def qkv_(i, t):
                free("qkv", i, t)
                pe.wait_ge(lnH_made, i + 1)
                pe.wait_ge(lnL_made, i + 1)
                if i == 0:
                    pe.wait_ge(WqkvL_made, 1)
                c = slice(t * P, (t + 1) * P)
                three(ring("qkv", i, t)[:, 0:3 * C], lnH[:, c], lnL[:, c], WqkvH[:], WqkvL[:]).then_inc(qkv_ps, 1)

            def kT(i):
                free("kT", i, 0)
                pe.wait_ge(qkn_made, i + 1)
                for t in range(T):
                    last = pe.transpose(ring("kT", i, 0)[:, t * P:(t + 1) * P], qkn[:, t, C:2 * C], ident[:])
                last.then_inc(kT_ps, 1)

            def qT(i):
                free("qT", i, 0)
                for t in range(T):
                    last = pe.transpose(ring("qT", i, 0)[:, t * P:(t + 1) * P], qkn[:, t, 0:C], ident[:])
                last.then_inc(qT_ps, 1)

            def ctxT():
                free("ctxT", 0, 0)
                pe.wait_ge(cxh_made, 1)
                for b in range(B):
                    last = pe.transpose(ring("ctxT", 0, 0)[0:CX, b * M:(b + 1) * M], cxh[:, b], ident[0:M, 0:M])
                last.then_inc(ctxT_ps, 1)

            def ctx_kv(n):
                free("ctx_kv", 0, n)
                pe.wait_ge(cT_made, 1)
                pe.wait_ge(WctxT_made, 1)
                for k in range(2):
                    last = pe.matmul(ring("ctx_kv", 0, n)[0:M, k * 2 * C:(k + 1) * 2 * C], cT[:, 2 * n + k], WctxT[:],
                                     start=True, stop=True)
                last.then_inc(ckv_ps, 1)

            def ctx_kT():
                free("ctx_kT", 0, 0)
                pe.wait_ge(ckn_made, 1)
                for b in range(B):
                    last = pe.transpose(ring("ctx_kT", 0, 0)[:, b * M:(b + 1) * M], ckn[:, b], ident[0:M, 0:M])
                last.then_inc(ckT_ps, 1)

            def score(i, n):
                g = KT * i + n
                if g >= 2:
                    pe.wait_ge(probs_made, g - 1)
                if g < 2:
                    pe.wait_ge(WctxT_made, 1)
                    pe.wait_ge(cbias_made, 1)
                pe.wait_ge(KL_made, i + 1)
                pe.wait_ge(QL_made, i + 1)
                for h in range(H):
                    if n < T:
                        c = slice(n * P, (n + 1) * P)
                        last = three(S_ps[g % 2][:, h], KH[i % 2][:, c], KL[i % 2][:, c], QH[i % 2][:, h], QL[i % 2][:, h])
                    else:
                        pe.wait_ge(cKL_made, 1)
                        last = three(S_ps[g % 2][0:M, h], cKH[:, i], cKL[:, i], QH[i % 2][:, h], QL[i % 2][:, h])
                last.then_inc(scores_ps, 1)

            def value(i, n):
                pe.wait_ge(probs_made, KT * i + n + 1)
                if i >= 1 and n == 0:
                    pe.wait_ge(oT_made, i)
                for h in range(H):
                    lo = 2 * C + h * D if n < T else C + h * D
                    v = qkv[i % 2][:, n, lo:lo + D] if n < T else ckv[:, i, lo:lo + D]
                    last = pe.matmul(O_ps[h * D:(h + 1) * D, :], v, Es[i % 2][n][:, h], start=(n == 0), stop=(n == KT - 1))
                if n == KT - 1:
                    last.then_inc(O_done, 1)

            def proj(i, t):
                free("proj", i, t)
                pe.wait_ge(oT_made, i + 1)
                pe.wait_ge(esum_made, i + 1)
                if i == 0:
                    pe.wait_ge(ones_made, 1)
                ps = ring("proj", i, t)
                c = slice(t * P, (t + 1) * P)
                pe.matmul(ps[:, 0:H * C], oT[:, c], WoT[:].rearrange("p h c -> p (h c)"), start=True, stop=True)
                for h in range(H):
                    last = pe.matmul(ps[:, (H + h) * C:(H + h + 1) * C], esum[i % 2][:, h, c], ones[:],
                                     start=True, stop=True)
                last.then_inc(proj_ps, 1)

            def l2T_(i):
                free("l2T", i, 0)
                pe.wait_ge(l2_made, i + 1)
                for t in range(T):
                    last = pe.transpose(ring("l2T", i, 0)[:, t * P:(t + 1) * P], l2[:, t], ident[:])
                last.then_inc(l2T_ps, 1)

            def gate(i):
                free("gate", i, 0)
                pe.wait_ge(l2T_made, i + 1)
                if i == 0:
                    pe.wait_ge(Wg_in, 16)
                for t in range(T):
                    c = slice(t * P, (t + 1) * P)
                    last = pe.matmul(ring("gate", i, 0)[:, c], l2T[:, c], Wg_sb[:], start=True, stop=True)
                last.then_inc(gate_ps, 1)

            def gateT(i):
                free("gateT", i, 0)
                pe.wait_ge(w_made, i + 1)
                pe.transpose(ring("gateT", i, 0)[0:T * E, 0:P], w[i % 2][:].rearrange("p t e -> p (t e)"),
                             ident[:]).then_inc(gateT_ps, 1)

            def bias(i):
                free("bias", i, 0)
                pe.wait_ge(wT_made, i + 1)
                if i == 0:
                    pe.wait_ge(blk_in, 16 * T)
                pe.matmul(ring("bias", i, 0)[:], wT[:], bias_blk[:].rearrange("p t c -> p (t c)"),
                          start=True, stop=True).then_inc(bias_ps, 1)

            def experts(kind, i, t, e0, done):
                free(kind, i, t)
                pe.wait_ge(l2L_made, i + 1)
                if i == 0:
                    pe.wait_ge(WeL_made, 1)
                c = slice(t * P, (t + 1) * P)
                rH, rL = (W[:, e0:e0 + EH].rearrange("p e c -> p (e c)") for W in (WeH, WeL))
                three(ring(kind, i, t)[:], l2H[:, c], l2L[:, c], rH, rL).then_inc(done, 1)

            for kind, i, t in steps:
                if kind == "weights":
                    weights()
                elif kind == "params":
                    params()
                elif kind == "constants":
                    constants()
                elif kind == "xT":
                    xT(i)
                elif kind == "qkv":
                    qkv_(i, t)
                elif kind == "kT":
                    kT(i)
                elif kind == "qT":
                    qT(i)
                elif kind == "ctxT":
                    ctxT()
                elif kind == "ctx_kv":
                    ctx_kv(t)
                elif kind == "ctx_kT":
                    ctx_kT()
                elif kind == "score":
                    score(i, t)
                elif kind == "value":
                    value(i, t)
                elif kind == "proj":
                    proj(i, t)
                elif kind == "l2T":
                    l2T_(i)
                elif kind == "gate":
                    gate(i)
                elif kind == "gateT":
                    gateT(i)
                elif kind == "bias":
                    bias(i)
                elif kind == "experts_low":
                    experts("experts_low", i, t, 0, low_ps)
                elif kind == "experts_high":
                    experts("experts_high", i, t, EH, high_ps)


_INS = ['x', 'ctx_768', 'mask_BxS2_bk0', 'L0_xattn_ln_x_g', 'L0_xattn_ln_x_b', 'L0_xattn_ln_l_g', 'L0_xattn_ln_l_b',
        'L0_xattn_qn_g', 'L0_xattn_kn_g', 'L0_xattn_Wq', 'L0_xattn_Wkv', 'L0_xattn_Wlkv', 'L0_xattn_Wo', 'L0_xattn_bo',
        'L0_ffn_W', 'L0_ffn_b', 'L0_ffn_Wg', 'L0_ffn_bg']
_OUTS = [((4, 512, 128), 'float32')]


def kernel(**inputs):
    import numpy as _np
    import concourse.bacc as _bacc
    from concourse import mybir as _mybir
    from concourse.bass_utils import run_bass_kernel_spmd as _run

    nc = _bacc.Bacc("TRN2", target_bir_lowering=False, num_devices=1)
    arrays, args = {}, []
    for name in _INS:
        a = _np.ascontiguousarray(inputs[name])
        arrays[f"in_{name}_dram"] = a
        args.append(nc.dram_tensor(f"in_{name}_dram", a.shape, _mybir.dt.from_np(a.dtype), kind="ExternalInput").ap())
    for i, (shape, dtype) in enumerate(_OUTS):
        dt = _mybir.dt.from_np(_np.dtype(dtype))
        args.append(nc.dram_tensor(f"out_{i}_dram", shape, dt, kind="ExternalOutput").ap())
    build(nc, *args)
    r = _run(nc, [arrays], core_ids=[0])
    got = tuple(r.results[0][f"out_{i}_dram"] for i in range(len(_OUTS)))
    return got[0]
```

```python
from contextlib import ExitStack

import concourse.bass as bass
from concourse import mybir

ALU = mybir.AluOpType
ACT = mybir.ActivationFunctionType
AX = mybir.AxisListType
F32 = mybir.dt.float32
F32R = mybir.dt.float32r
U32 = mybir.dt.uint32
U8 = mybir.dt.uint8

P = 128
LN_EPS = 1e-5
RMS_EPS = 1e-8
MASKED = 1e30
SAFE_EXP = 60.0
RING = 6


BEFORE = """
     P.warm 1 17   P.weights 1 0   P.xT 1 0   P.warm 1 11   V.stats1 1 0   V.stats1 2 0   V.ones 1 0
    G.experts_in 1 0   G.rstd1 1 0   V.zeros 1 0   V.apply1 1 0   G.rstd1 2 0   V.apply1 2 0   V.weights 1 0
    A.weights 1 0   V.stats1 3 0   V.ss 1 0   V.shift 1 0   V.gain 1 0   A.lnT 1 0   G.lnL 1 0   P.xT 2 0
    A.lnT 2 0   A.qkv 1 0   G.lnL 2 0   P.qkv 1 0   P.qkv 1 1   A.qkv 1 1   A.sq 1 0   P.warm 1 4   P.qkv 2 0
    A.weights2 1 0   A.qkv 2 0   P.weights2 1 0   P.qkv 2 1   A.qkv 2 1   A.sq 2 0   G.rstd1 3 0   G.rqk 1 0
    G.rqk 2 0   V.ss 2 0   V.qkn 1 0   P.kT 1 0   P.qT 1 0   A.QH 1 0   A.KS 1 0   V.apply1 3 0   V.qkn 2 0
    V.QL 1 0   V.KL 1 0   P.warm 1 14   P.xT 3 0   P.warm 1 1   P.kT 2 0   P.qT 2 0   P.warm 1 12   G.lnL 3 0
    A.KS 2 0   A.lnT 3 0   A.QH 2 0   V.KL 2 0
"""
PERIOD = """
     P.low -2 0   P.score 0 0   V.ctx_stats + 0   V.wT -2 0   V.QL 1 0   P.gateT -2 0   A.exp 0 0   A.low -2 0
    P.proj -1 0   P.proj -1 1   V.x2 -1 0   V.x2b -2 0   G.ctx_rstd + 0   G.rstd2 -1 0   G.ctx_rk + 0
    V.stats2 -1 0   V.high -2 0   V.mask + 0   V.ctx_apply + 0   V.apply2 -1 0   V.split + 0   G.e01 0 0
    G.rqk 2 0   P.bias -2 0   P.qkv 2 0   P.high -2 0   P.value 0 0   P.score 0 1   P.qkv 2 1   P.score 0 2
    P.ctxT + 0   A.qkv 2 0   A.exp 0 1   V.ctx_ss + 0   V.ss 2 0   V.high -2 1   V.ctx_kn + 0   P.ctx_kv + 0
    P.low -2 1   P.high -2 1   P.ctx_kv + 1   P.l2T -1 0   A.qkv 2 1   A.ctxT + 0   A.sq 2 0   A.exp 0 2
    A.l2T -1 0   A.ctx_kv + 0   A.ctx_kv + 1   P.score 0 3   P.value 0 1   P.ctx_kT + 0   P.maskT + 0
    P.gate -1 0   V.stats1 3 0   V.cbias + 0   V.ctx_KL + 0   V.logits -1 0   A.exp 0 3   A.low -2 1
    A.ctx_KS + 0   A.gexp -1 0   A.ctx_KS + 1   A.exp 0 4   V.qkn 2 0   G.rstd1 3 0   G.xbo 0 0   G.sum -2 0
    G.l2L -1 0   V.apply1 3 0   V.e23 0 0   V.top -1 0   P.ctx_kT + 1   P.value 0 2   P.score 0 4   P.kT 2 0
    A.KS 2 0   V.esum1 0 0   V.ctx_KL + 1   V.KL 2 0   G.sum -2 1   G.lnL 3 0   P.value 0 3   P.value 0 4
    P.xT 3 0   P.qT 2 0   V.esum2 0 0   A.oT 0 0   A.lnT 3 0   A.QH 2 0
"""
AFTER = """
     V.wT -2 0   P.gateT -2 0   P.proj -1 0   P.proj -1 1   P.bias -2 0   P.low -2 0   P.high -2 0   P.low -2 1
    V.x2 -1 0   V.stats2 -1 0   G.rstd2 -1 0   V.apply2 -1 0   V.x2b -2 0   V.high -2 0   G.l2L -1 0
    G.sum -2 0   P.l2T -1 0   A.l2T -1 0   A.low -2 0   P.high -2 1   P.gate -1 0   V.logits -1 0   A.gexp -1 0
    A.low -2 1   V.top -1 0   V.wT -1 0   V.high -2 1   G.sum -2 1   P.low -1 0   P.high -1 0   P.gateT -1 0
    A.low -1 0   V.x2b -1 0   V.high -1 0   G.sum -1 0   A.low -1 1   P.bias -1 0   P.low -1 1   P.high -1 1
    V.high -1 1   G.sum -1 1
"""


def schedule(units):
    steps = []
    for period in range(-1, units + 1):
        text = (BEFORE if period < 0 else AFTER if period == units else PERIOD).split()
        while text:
            (engine, kind), offset, index = text.pop(0).split("."), text.pop(0), int(text.pop(0))
            if offset == "+":
                if period == 0:
                    steps.append((engine, kind, 0, index))
            elif 0 <= period + int(offset) < units:
                steps.append((engine, kind, period + int(offset), index))
    return steps


def build(nc, x, ctx, mask, lxg, lxb, llg, llb, qng, kng, Wq, Wkv, Wlkv, Wo, bo, We, be, Wg, bg, out):
    B, S, C = x.shape
    _, M, CX = ctx.shape
    E = We.shape[0]
    D = qng.shape[0]
    H = C // D
    T = S // P
    KT = T + 1
    SCALE = float(D) ** -0.5
    EH = E // 2
    HT = T // 2
    N = HT * P
    U = 2 * B
    steps = schedule(U)

    def tiles(u):
        return range(HT * (u % 2), HT * (u % 2) + HT)

    def cols_of(u):
        return slice(N * (u % 2), N * (u % 2) + N)

    def local(n):
        return slice(n * P, (n + 1) * P)

    jobs = [(kind, u, n) for engine, kind, u, n in steps if engine == "P" and kind not in ("value", "warm")]
    slot = {job: n % RING for n, job in enumerate(jobs)}
    before = {job: jobs[n - RING] for n, job in enumerate(jobs) if n >= RING}

    with ExitStack() as st:
        def sb(name, shape, dt=F32):
            return st.enter_context(nc.sbuf_tensor(name, shape, dt))

        def two(name, shape, dt=F32):
            return [sb(f"{name}{n}", shape, dt) for n in range(2)]

        def sem(name):
            return st.enter_context(nc.semaphore(name))

        x_sb = sb("x_sb", [P, B, T, C])
        ctx_sb = sb("ctx_sb", [M, B, CX])
        mask8 = sb("mask8", [B, M], U8)
        maskf = sb("maskf", [B, M])
        ln_cols = sb("ln_cols", [P, 2])
        qk_cols = sb("qk_cols", [P, 2])
        ctx_cols = sb("ctx_cols", [CX, 2])
        bo_b = sb("bo_b", [P, C])
        bg_b = sb("bg_b", [P, E])
        gq_b = sb("gq_b", [P, D])
        gk_b = sb("gk_b", [P, D])
        Wq_sb = sb("Wq_sb", [P, C])
        Wlkv_sb = sb("Wlkv_sb", [P, 2, C])
        Wkv_sb = sb("Wkv_sb", [P, 2, CX])
        Wo_sb = sb("Wo_sb", [P, C])
        We_sb = sb("We_sb", [P, E, C])
        WeH = sb("WeH", [P, E, C], F32R)
        WeL = sb("WeL", [P, E, C], F32R)
        WqkvH = sb("WqkvH", [P, 3 * C], F32R)
        WqkvL = sb("WqkvL", [P, 3 * C], F32R)
        WctxT = sb("WctxT", [CX, 2 * C])
        WoT = sb("WoT", [P, H, C])
        Wg_sb = sb("Wg_sb", [P, P])
        bias_blk = sb("bias_blk", [P, HT, C])
        ident = sb("ident", [P, P])
        ones = sb("ones", [P, P])
        half = sb("half", [P, HT * 2 * H])
        act_warm = sb("act_warm", [P, 1])
        iota_e = sb("iota_e", [P, E])
        gain = sb("gain", [P, 1])
        gprod = sb("gprod", [P, D])
        gmax = sb("gmax", [P, 1])
        shift0 = sb("shift0", [P, 1])
        shift = sb("shift", [P, 1])
        mbias = sb("mbias", [M, B])
        cbias = sb("cbias", [M, B])
        cstat = sb("cstat", [M, B, 6])
        cmv = sb("cmv", [M, B, 2])
        cvar = sb("cvar", [M, B])
        crstd = sb("crstd", [M, B])
        cxh = sb("cxh", [M, B, CX])
        cT = sb("cT", [CX, B, M])
        ckv = sb("ckv", [M, B, 2 * C])
        csq = sb("csq", [M, B, C])
        css = sb("css", [M, B * H])
        cms = sb("cms", [M, B * H])
        crk = sb("crk", [M, B * H])
        ckn = sb("ckn", [M, B, H, 2, D])
        cKS = sb("cKS", [P, B, H, M], F32R)
        stat1 = two("stat1_", [P, HT, 6])
        mv1 = two("mv1_", [P, HT, 2])
        var1 = two("var1_", [P, HT])
        rstd1 = two("rstd1_", [P, HT])
        xh = two("xh", [P, HT, C])
        lnT = two("lnT", [P, N])
        lnH = two("lnH", [P, N], F32R)
        lnL = two("lnL", [P, N], F32R)
        qkv = two("qkv", [P, T, 3 * C])
        sq = two("sq", [P, HT, 2 * C])
        ss = two("ss", [P, HT, 2 * H])
        ms = two("ms", [P, HT, 2 * H])
        rqk = two("rqk", [P, HT, 2 * H])
        qkn = two("qkn", [P, HT, 2 * H, 2, D])
        KS = two("KS", [P, H, S], F32R)
        QH = two("QH", [P, H, S], F32R)
        QL = two("QL", [P, H, S], F32R)
        probs = [[sb(f"probs{n}_{k}", [P, H, N]) for k in range(KT)] for n in range(2)]
        e01 = two("e01_", [P, H, N])
        esum = two("esum", [P, H, N])
        oT = two("oT", [P, N])
        xbo = two("xbo", [P, HT, C])
        rden = sb("rden", [P, HT, H])
        x2a = sb("x2a", [P, HT, C])
        x2 = two("x2_", [P, HT, C])
        x2b = two("x2b_", [P, HT, C])
        stat2 = two("stat2_", [P, HT, 6])
        mv2 = two("mv2_", [P, HT, 2])
        var2 = two("var2_", [P, HT])
        rstd2 = two("rstd2_", [P, HT])
        l2 = two("l2_", [P, HT, C])
        l2T = two("l2T", [P, N])
        l2H = two("l2H", [P, N], F32R)
        l2L = two("l2L", [P, N], F32R)
        lg = two("lg", [P, HT, E])
        nmx = two("nmx", [P, HT])
        lgs = two("lgs", [P, HT, E])
        eg = two("eg", [P, HT, E])
        esm = sb("esm", [P, HT])
        erc = sb("erc", [P, HT])
        top = sb("top", [P, HT, 8])
        topi = sb("topi", [P, HT, 8], U32)
        topf = sb("topf", [P, HT, 2])
        eq1 = sb("eq1", [P, HT, E])
        eq2 = sb("eq2", [P, HT, E])
        er = sb("er", [P, HT, E])
        w = two("w", [P, HT, E])
        wT = sb("wT", [P, P])
        scaled = two("scaled", [P, EH, C])
        pair = sb("pair", [P, EH // 2, C])
        low = sb("low", [P, C])
        acc = two("acc", [P, C])
        part = [sb(f"part{n}", [P, C]) for n in range(EH - 1)]
        res = two("res", [P, HT, C])

        O_ps = [st.enter_context(nc.psum_tensor(f"O_ps{n}", [P, S], F32)) for n in range(2)]
        R_ps = [st.enter_context(nc.psum_tensor(f"R_ps{n}", [P, S], F32)) for n in range(RING)]

        def ring(kind, u, n):
            return R_ps[slot[(kind, u, n)]]

        x_in = [sem(f"x_in{n}") for n in range(B)]
        Wlat_in, Wo_in, Wctx_in, We_in, Wg_in, blk_in = (
            sem("Wlat_in"), sem("Wo_in"), sem("Wctx_in"), sem("We_in"), sem("Wg_in"), sem("blk_in"))
        ln_in, qk_in, ctx_cols_in, mask_in, gains_in, bias_in, ctx_in = (
            sem("ln_in"), sem("qk_in"), sem("ctx_cols_in"), sem("mask_in"), sem("gains_in"), sem("bias_in"), sem("ctx_in"))
        stored = [sem(f"stored{n}") for n in range(2)]
        ident_zeroed, ident_made, half_made, ones_made, iota_made = (
            sem("ident_zeroed"), sem("ident_made"), sem("half_made"), sem("ones_made"), sem("iota_made"))
        Wg_zeroed, blk_zeroed, pads_zeroed = sem("Wg_zeroed"), sem("blk_zeroed"), sem("pads_zeroed")
        mask_made, maskT_done, gain_made, shift_made, cbias_made = (
            sem("mask_made"), sem("maskT_done"), sem("gain_made"), sem("shift_made"), sem("cbias_made"))
        Wlat_done, Wctx_done = sem("Wlat_done"), sem("Wctx_done")
        WqkvH_made, WqkvL_made, WoT_made, WctxT_made = sem("WqkvH_made"), sem("WqkvL_made"), sem("WoT_made"), sem("WctxT_made")
        WeH_made, WeL_made = sem("WeH_made"), sem("WeL_made")
        cmv_made, crstd_made, cxh_made, ctxT_done, cT_made = (
            sem("cmv_made"), sem("crstd_made"), sem("cxh_made"), sem("ctxT_done"), sem("cT_made"))
        ckv_done, ckv_made, css_made, crk_made, ckn_made, ckT_done, cKS_made, cKL_made = (
            sem("ckv_done"), sem("ckv_made"), sem("css_made"), sem("crk_made"), sem("ckn_made"), sem("ckT_done"),
            sem("cKS_made"), sem("cKL_made"))
        mv1_made, rstd1_made, xh_made, xT_done, lnT_made, lnL_made = (
            sem("mv1_made"), sem("rstd1_made"), sem("xh_made"), sem("xT_done"), sem("lnT_made"), sem("lnL_made"))
        qkv_done, qkv_made, sq_made, ss_made, rqk_made, qkn_made = (
            sem("qkv_done"), sem("qkv_made"), sem("sq_made"), sem("ss_made"), sem("rqk_made"), sem("qkn_made"))
        kT_done, qT_done, KS_made, QH_made, KL_made, QL_made = (
            sem("kT_done"), sem("qT_done"), sem("KS_made"), sem("QH_made"), sem("KL_made"), sem("QL_made"))
        scores_done, probs_made, e01_made, esum_made, O_done, oT_made = (
            sem("scores_done"), sem("probs_made"), sem("e01_made"), sem("esum_made"), sem("O_done"), sem("oT_made"))
        xbo_made, proj_done, x2_made, mv2_made, rstd2_made, l2_made = (
            sem("xbo_made"), sem("proj_done"), sem("x2_made"), sem("mv2_made"), sem("rstd2_made"), sem("l2_made"))
        l2T_done, l2T_made, l2L_made, gate_done, lg_made, lgs_made, eg_made = (
            sem("l2T_done"), sem("l2T_made"), sem("l2L_made"), sem("gate_done"), sem("lg_made"), sem("lgs_made"), sem("eg_made"))
        w_made, gateT_done, wT_made, bias_done, x2b_made = (
            sem("w_made"), sem("gateT_done"), sem("wT_made"), sem("bias_done"), sem("x2b_made"))
        low_done, high_done, scaled_made, acc_made, res_made = (
            sem("low_done"), sem("high_done"), sem("scaled_made"), sem("acc_made"), sem("res_made"))
        dve_step, pool_step = sem("dve_step"), sem("pool_step")

        RELEASED = {
            "weights": lambda u, n: (WqkvL_made, 1),
            "weights2": lambda u, n: (WctxT_made, 1),
            "maskT": lambda u, n: (cbias_made, 1),
            "score": lambda u, n: (probs_made, KT * u + n + 1),
            "xT": lambda u, n: (lnT_made, u + 1),
            "qkv": lambda u, n: (qkv_made, HT * u + n + 1),
            "kT": lambda u, n: (KL_made, u + 1),
            "qT": lambda u, n: (QL_made, u + 1),
            "ctxT": lambda u, n: (cT_made, 1),
            "ctx_kv": lambda u, n: (ckv_made, n + 1),
            "ctx_kT": lambda u, n: (cKL_made, n + 1),
            "proj": lambda u, n: (x2_made, HT * u + n + 1),
            "l2T": lambda u, n: (l2T_made, u + 1),
            "gate": lambda u, n: (lg_made, u + 1),
            "gateT": lambda u, n: (wT_made, u + 1),
            "bias": lambda u, n: (x2b_made, u + 1),
            "low": lambda u, n: (scaled_made, HT * u + n + 1),
            "high": lambda u, n: (acc_made, HT * u + n + 1),
        }

        def row(v):
            return v.rearrange("(a d) -> a d", a=1)

        def column(v):
            return v.rearrange("(d a) -> d a", a=1)

        def walk(engine, does):
            for who, kind, u, n in steps:
                if who == engine:
                    does[kind](u, n)

        block = st.enter_context(nc.Block())

        @block.sync
        def _(sp):
            sp.dma_start(x_sb[:, 0], x[0].rearrange("(p t) c -> p t c", t=T)).then_inc(x_in[0], 16)
            for n, v in enumerate((llg, llb)):
                sp.dma_start(ln_cols[:, n:n + 1], column(v)).then_inc(ln_in, 16)
            for n, v in enumerate((qng, kng)):
                for h in range(2):
                    sp.dma_start(qk_cols[h * D:(h + 1) * D, n:n + 1], column(v)).then_inc(qk_in, 16)
            sp.dma_start(gq_b[:], row(qng).to_broadcast([P, D])).then_inc(gains_in, 16)
            sp.dma_start(gk_b[:], row(kng).to_broadcast([P, D])).then_inc(gains_in, 16)
            sp.dma_start(x_sb[:, 1], x[1].rearrange("(p t) c -> p t c", t=T)).then_inc(x_in[1], 16)
            sp.dma_start(ctx_sb[:], ctx.rearrange("b m c -> m b c")).then_inc(ctx_in, 16)
            for n, v in enumerate((lxg, lxb)):
                sp.dma_start(ctx_cols[:, n:n + 1], column(v)).then_inc(ctx_cols_in, 16)
            sp.dma_start(mask8[:], mask).then_inc(mask_in, 16)
            sp.dma_start(bo_b[:], row(bo).to_broadcast([P, C])).then_inc(bias_in, 16)
            sp.dma_start(bg_b[:], row(bg).to_broadcast([P, E])).then_inc(bias_in, 16)
            sp.wait_ge(Wg_zeroed, 1)
            sp.dma_start(Wg_sb[:, 0:E], Wg).then_inc(Wg_in, 16)
            sp.wait_ge(blk_zeroed, 1)
            for t in range(HT):
                sp.dma_start(bias_blk[E * t:E * (t + 1), t], be).then_inc(blk_in, 16)
            for i in range(2, B):
                sp.dma_start(x_sb[:, i], x[i].rearrange("(p t) c -> p t c", t=T)).then_inc(x_in[i], 16)
            for u in range(U):
                dst = out[u // 2].rearrange("(p t) c -> p t c", t=T)[:, tiles(u)[0]:tiles(u)[-1] + 1]
                if u < U - 1:
                    sp.wait_ge(res_made, HT * (u + 1))
                    sp.dma_start(dst, res[u % 2][:]).then_inc(stored[u % 2], 16)
                else:
                    for n in range(HT):
                        sp.wait_ge(res_made, HT * u + n + 1)
                        sp.dma_start(dst[:, n], res[u % 2][:, n]).then_inc(stored[u % 2], 16)
            sp.wait_ge(stored[0], 16 * B)
            sp.wait_ge(stored[1], 16 * (B - 1 + HT))

        @block.gpsimd
        def _(pool):
            count = [0]

            def step(ins):
                count[0] += 1
                ins.then_inc(pool_step, 1)
                pool.wait_ge(pool_step, count[0])

            pool.memset(ident[:], 0.0).then_inc(ident_zeroed, 1)
            pool.wait_ge(ident_zeroed, 1)
            pool.affine_select(out=ident[:], in_=ident[:], compare_op=ALU.not_equal, fill=1.0, base=0,
                               pattern=[[-1, P]], channel_multiplier=1).then_inc(ident_made, 1)
            pool.memset(half[:], -0.5).then_inc(half_made, 1)

            def experts_in_(u, n):
                pool.dma_start(We_sb[:], We.rearrange("e h o -> h e o")).then_inc(We_in, 16)
                pool.memset(Wg_sb[:], 0.0).then_inc(Wg_zeroed, 1)
                pool.memset(bias_blk[:], 0.0).then_inc(blk_zeroed, 1)
                pool.iota(iota_e[:], pattern=[[1, E]], base=0, channel_multiplier=0,
                          allow_small_or_imprecise_dtypes=True).then_inc(iota_made, 1)

            def rstd1_(u, n):
                k = u % 2
                pool.wait_ge(mv1_made, u + 1)
                step(pool.tensor_scalar(var1[k][:], mv1[k][:, :, 1], 1.0 + LN_EPS, LN_EPS * LN_EPS, ALU.mult, ALU.add))
                pool.tensor_tensor(rstd1[k][:], var1[k][:], half[:, 0:HT], ALU.pow).then_inc(rstd1_made, 1)

            def lnL_(u, n):
                k = u % 2
                pool.wait_ge(lnT_made, u + 1)
                if u >= 2:
                    pool.wait_ge(qkv_done, HT * (u - 1))
                pool.tensor_tensor(lnL[k][:], lnT[k][:], lnH[k][:].bitcast(F32), ALU.subtract).then_inc(lnL_made, 1)

            def rqk_(u, n):
                k = u % 2
                pool.wait_ge(ss_made, u + 1)
                if u >= 2:
                    pool.wait_ge(qkn_made, u - 1)
                step(pool.tensor_scalar(ms[k][:], ss[k][:], 1.0 / D, RMS_EPS * RMS_EPS, ALU.mult, ALU.max))
                pool.tensor_tensor(rqk[k][:], ms[k][:], half[:].rearrange("p (t g) -> p t g", g=2 * H),
                                   ALU.pow).then_inc(rqk_made, 1)

            def ctx_rstd_(u, n):
                pool.wait_ge(cmv_made, 1)
                step(pool.tensor_scalar(cvar[:], cmv[:, :, 1], 1.0, LN_EPS, ALU.mult, ALU.add))
                pool.tensor_tensor(crstd[:], cvar[:], half[0:M, 0:B], ALU.pow).then_inc(crstd_made, 1)

            def ctx_rk_(u, n):
                pool.wait_ge(css_made, 1)
                step(pool.tensor_scalar(cms[:], css[:], 1.0 / D, RMS_EPS * RMS_EPS, ALU.mult, ALU.max))
                pool.tensor_tensor(crk[:], cms[:], half[0:M, 0:B * H], ALU.pow).then_inc(crk_made, 1)

            def e01_(u, n):
                pool.wait_ge(probs_made, KT * u + 2)
                if u >= 2:
                    pool.wait_ge(esum_made, u - 1)
                pool.tensor_tensor(e01[u % 2][:], probs[u % 2][0][:], probs[u % 2][1][:], ALU.add).then_inc(e01_made, 1)

            def xbo_(u, n):
                pool.wait_ge(bias_in, 32)
                pool.wait_ge(x_in[u // 2], 16)
                if u >= 2:
                    pool.wait_ge(x2_made, HT * (u - 1))
                pool.tensor_tensor(xbo[u % 2][:], x_sb[:, u // 2, tiles(u)[0]:tiles(u)[-1] + 1],
                                   bo_b[:].unsqueeze(1).to_broadcast([P, HT, C]), ALU.add).then_inc(xbo_made, 1)

            def rstd2_(u, n):
                k = u % 2
                pool.wait_ge(mv2_made, u + 1)
                step(pool.tensor_scalar(var2[k][:], mv2[k][:, :, 1], 1.0, LN_EPS, ALU.mult, ALU.add))
                pool.tensor_tensor(rstd2[k][:], var2[k][:], half[:, 0:HT], ALU.pow).then_inc(rstd2_made, 1)

            def l2L_(u, n):
                k = u % 2
                pool.wait_ge(l2T_made, u + 1)
                if u >= 2:
                    pool.wait_ge(low_done, HT * (u - 1))
                    pool.wait_ge(high_done, HT * (u - 1))
                pool.tensor_tensor(l2L[k][:], l2T[k][:], l2H[k][:].bitcast(F32), ALU.subtract).then_inc(l2L_made, 1)

            def sum_(u, n):
                m = HT * u + n
                pool.wait_ge(scaled_made, m + 1)
                step(pool.tensor_tensor(pair[:], scaled[m % 2][:, 0:EH // 2], scaled[m % 2][:, EH // 2:EH], ALU.add))
                step(pool.tensor_tensor(low[:], pair[:, 0], pair[:, 1], ALU.add))
                pool.wait_ge(acc_made, m + 1)
                if n == 0 and u >= 2:
                    pool.wait_ge(stored[u % 2], 16 * (u // 2))
                pool.tensor_tensor(res[u % 2][:, n], low[:], acc[m % 2][:], ALU.add).then_inc(res_made, 1)

            walk("G", dict(experts_in=experts_in_, rstd1=rstd1_, lnL=lnL_, rqk=rqk_, ctx_rstd=ctx_rstd_, ctx_rk=ctx_rk_,
                           e01=e01_, xbo=xbo_, rstd2=rstd2_, l2L=l2L_, sum=sum_))

        @block.scalar
        def _(act):
            act.dma_start(Wlkv_sb[:], Wlkv.rearrange("(a o) c -> o a c", a=2)).then_inc(Wlat_in, 16)
            act.dma_start(Wq_sb[:], Wq).then_inc(Wlat_in, 16)
            act.dma_start(Wo_sb[:], Wo).then_inc(Wo_in, 16)
            act.dma_start(Wkv_sb[:], Wkv.rearrange("(a o) c -> o a c", a=2)).then_inc(Wctx_in, 16)

            act.wait_ge(half_made, 1)
            act.activation(act_warm[:], half[:, 0:1], ACT.Exp)

            def weights_(u, n):
                act.wait_ge(Wlat_done, 1)
                act.copy(WqkvH[:], ring("weights", 0, 0)[:, 0:3 * C]).then_inc(WqkvH_made, 1)

            def weights2_(u, n):
                act.wait_ge(Wctx_done, 1)
                act.wait_ge(pads_zeroed, 1)
                for h in range(H):
                    r = slice(h * D, (h + 1) * D)
                    last = act.copy(WoT[r, h], ring("weights2", 0, 0)[r, 0:C])
                last.then_inc(WoT_made, 1)
                act.copy(WctxT[:], ring("weights2", 0, 0)[0:CX, C:3 * C]).then_inc(WctxT_made, 1)

            def lnT_(u, n):
                k = u % 2
                act.wait_ge(xT_done, u + 1)
                act.wait_ge(ln_in, 32)
                if u >= 2:
                    act.wait_ge(qkv_done, HT * (u - 1))
                    act.wait_ge(lnL_made, u - 1)
                for dst in (lnT[k], lnH[k]):
                    last = act.activation(dst[:], ring("xT", u, 0)[:, 0:N], ACT.Identity, bias=ln_cols[:, 1:2],
                                          scale=ln_cols[:, 0:1])
                last.then_inc(lnT_made, 1)

            def qkv_(u, n):
                i = u // 2
                act.wait_ge(qkv_done, HT * u + n + 1)
                if i >= 2:
                    act.wait_ge(O_done, 2 * (i - 1))
                act.copy(qkv[i % 2][:, tiles(u)[n]], ring("qkv", u, n)[:, 0:3 * C]).then_inc(qkv_made, 1)

            def sq_(u, n):
                act.wait_ge(qkv_made, HT * (u + 1))
                if u >= 2:
                    act.wait_ge(ss_made, u - 1)
                act.activation(sq[u % 2][:], qkv[u // 2 % 2][:, tiles(u)[0]:tiles(u)[-1] + 1, 0:2 * C],
                               ACT.Square).then_inc(sq_made, 1)

            def KS_(u, n):
                i = u // 2
                act.wait_ge(kT_done, u + 1)
                act.wait_ge(gain_made, 1)
                if i >= 2:
                    act.wait_ge(scores_done, 2 * KT * (i - 1))
                act.activation(KS[i % 2][:, :, cols_of(u)], ring("kT", u, 0)[:].rearrange("p (h s) -> p h s", h=H),
                               ACT.Identity, scale=gain[:, 0:1]).then_inc(KS_made, 1)

            def QH_(u, n):
                act.wait_ge(qT_done, u + 1)
                if u >= 4:
                    act.wait_ge(scores_done, KT * (u - 3))
                act.copy(QH[u // 2 % 2][:, :, cols_of(u)],
                         ring("qT", u, 0)[:].rearrange("p (h s) -> p h s", h=H)).then_inc(QH_made, 1)

            def ctxT_(u, n):
                act.wait_ge(ctxT_done, 1)
                act.wait_ge(ctx_cols_in, 32)
                act.activation(cT[:].rearrange("c b m -> c (b m)"), ring("ctxT", 0, 0)[0:CX, 0:B * M], ACT.Identity,
                               bias=ctx_cols[:, 1:2], scale=ctx_cols[:, 0:1]).then_inc(cT_made, 1)

            def ctx_kv_(u, n):
                act.wait_ge(ckv_done, n + 1)
                act.copy(ckv[:, 2 * n:2 * n + 2].rearrange("m b c -> m (b c)"),
                         ring("ctx_kv", 0, n)[0:M, :]).then_inc(ckv_made, 1)

            def ctx_KS_(u, n):
                act.wait_ge(ckT_done, n + 1)
                act.wait_ge(gain_made, 1)
                act.activation(cKS[:, 2 * n:2 * n + 2].rearrange("p b h m -> p (b h m)"),
                               ring("ctx_kT", 0, n)[:, 0:2 * H * M], ACT.Identity,
                               scale=gain[:, 0:1]).then_inc(cKS_made, 1)

            def exp_(u, n):
                k = u % 2
                act.wait_ge(scores_done, KT * u + n + 1)
                act.wait_ge(shift_made, 1)
                if u >= 2 and n == 0:
                    act.wait_ge(O_done, u - 1)
                    act.wait_ge(esum_made, u - 1)
                ps = ring("score", u, n)[:].rearrange("p (h s) -> p h s", h=H)
                if n < T:
                    last = act.activation(probs[k][n][:], ps, ACT.Exp, bias=shift[:, 0:1])
                else:
                    act.wait_ge(cbias_made, 1)
                    last = act.activation(probs[k][n][0:M], ps[0:M], ACT.Exp, bias=cbias[:, u // 2:u // 2 + 1])
                last.then_inc(probs_made, 1)

            def oT_(u, n):
                act.wait_ge(O_done, u + 1)
                if u >= 2:
                    act.wait_ge(proj_done, HT * (u - 1))
                act.copy(oT[u % 2][:], O_ps[u % 2][:, 0:N]).then_inc(oT_made, 1)

            def l2T_(u, n):
                k = u % 2
                act.wait_ge(l2T_done, u + 1)
                if u >= 2:
                    act.wait_ge(gate_done, u - 1)
                    act.wait_ge(low_done, HT * (u - 1))
                    act.wait_ge(high_done, HT * (u - 1))
                    act.wait_ge(l2L_made, u - 1)
                for dst in (l2T[k], l2H[k]):
                    last = act.copy(dst[:], ring("l2T", u, 0)[:, 0:N])
                last.then_inc(l2T_made, 1)

            def gexp_(u, n):
                act.wait_ge(lgs_made, u + 1)
                if u >= 2:
                    act.wait_ge(w_made, u - 1)
                act.activation(eg[u % 2][:], lgs[u % 2][:], ACT.Exp).then_inc(eg_made, 1)

            def low_(u, n):
                m = HT * u + n
                act.wait_ge(low_done, m + 1)
                act.wait_ge(w_made, u + 1)
                if m >= 2:
                    act.wait_ge(res_made, m - 1)
                ps = ring("low", u, n)[:].rearrange("p (e c) -> p e c", e=EH)
                for e in range(EH):
                    last = act.activation(scaled[m % 2][:, e], ps[:, e], ACT.Copy, scale=w[u % 2][:, n, e:e + 1])
                last.then_inc(scaled_made, 1)

            walk("A", dict(weights=weights_, weights2=weights2_, lnT=lnT_, qkv=qkv_, sq=sq_, KS=KS_, QH=QH_,
                           ctxT=ctxT_, ctx_kv=ctx_kv_, ctx_KS=ctx_KS_, exp=exp_, oT=oT_, l2T=l2T_, gexp=gexp_, low=low_))

        @block.vector
        def _(dve):
            count = [0]

            def step(ins):
                count[0] += 1
                ins.then_inc(dve_step, 1)
                return count[0]

            def ones_(u, n):
                dve.memset(ones[:], 1.0).then_inc(ones_made, 1)

            def zeros_(u, n):
                dve.memset(WoT[:], 0.0)
                dve.memset(wT[:], 0.0).then_inc(pads_zeroed, 1)

            def gain_(u, n):
                dve.wait_ge(qk_in, 64)
                dve.scalar_tensor_tensor(gain[:], qk_cols[:, 0:1], SCALE, qk_cols[:, 1:2], ALU.mult,
                                         ALU.mult).then_inc(gain_made, 1)

            def shift_(u, n):
                dve.wait_ge(gains_in, 32)
                dve.wait_ge(dve_step, step(dve.tensor_tensor(gprod[:], gq_b[:], gk_b[:], ALU.mult)))
                dve.wait_ge(dve_step, step(dve.tensor_reduce(gmax[:], gprod[:], AX.X, ALU.max, apply_absolute_value=True)))
                dve.wait_ge(dve_step, step(dve.tensor_scalar(shift0[:], gmax[:], -D * SCALE, SAFE_EXP, ALU.mult, ALU.add)))
                dve.tensor_scalar(shift[:], shift0[:], 0.0, None, ALU.min).then_inc(shift_made, 1)

            def mask_(u, n):
                dve.wait_ge(mask_in, 16)
                dve.tensor_copy(maskf[:], mask8[:]).then_inc(mask_made, 1)

            def cbias_(u, n):
                dve.wait_ge(maskT_done, 1)
                dve.wait_ge(dve_step, step(dve.tensor_scalar(mbias[:], ring("maskT", 0, 0)[0:M, 0:B], 1.0, MASKED,
                                                             ALU.subtract, ALU.mult)))
                dve.wait_ge(shift_made, 1)
                dve.tensor_scalar(cbias[:], mbias[:], shift[0:M, 0:1], None, ALU.add).then_inc(cbias_made, 1)

            def weights_(u, n):
                dve.wait_ge(WqkvH_made, 1)
                dve.tensor_tensor(WqkvL[:], ring("weights", 0, 0)[:, 0:3 * C], WqkvH[:].bitcast(F32),
                                  ALU.subtract).then_inc(WqkvL_made, 1)

            def split_(u, n):
                dve.wait_ge(We_in, 16)
                dve.tensor_copy(WeH[:], We_sb[:]).then_inc(WeH_made, 1)
                dve.wait_ge(WeH_made, 1)
                dve.tensor_tensor(WeL[:], We_sb[:], WeH[:].bitcast(F32), ALU.subtract).then_inc(WeL_made, 1)

            def stats1_(u, n):
                k = u % 2
                dve.wait_ge(x_in[u // 2], 16)
                for m, t in enumerate(tiles(u)):
                    last = dve.bn_stats(stat1[k][:, m], x_sb[:, u // 2, t])
                dve.wait_ge(dve_step, step(last))
                for m in range(HT):
                    last = dve.bn_aggr(mv1[k][:, m], stat1[k][:, m])
                last.then_inc(mv1_made, 1)

            def apply1_(u, n):
                k = u % 2
                dve.wait_ge(rstd1_made, u + 1)
                if u >= 2:
                    dve.wait_ge(xT_done, u - 1)
                for m, t in enumerate(tiles(u)):
                    last = dve.tensor_scalar(xh[k][:, m], x_sb[:, u // 2, t], mv1[k][:, m, 0:1], rstd1[k][:, m:m + 1],
                                             ALU.subtract, ALU.mult)
                last.then_inc(xh_made, 1)

            def ss_(u, n):
                k = u % 2
                dve.wait_ge(sq_made, u + 1)
                if u >= 2:
                    dve.wait_ge(rqk_made, u - 1)
                dve.tensor_reduce(ss[k][:], sq[k][:].rearrange("p t (g d) -> p t g d", d=D), AX.X,
                                  ALU.add).then_inc(ss_made, 1)

            def qkn_(u, n):
                k = u % 2
                dve.wait_ge(rqk_made, u + 1)
                if u >= 2:
                    dve.wait_ge(kT_done, u - 1)
                    dve.wait_ge(qT_done, u - 1)
                src = qkv[u // 2 % 2][:, tiles(u)[0]:tiles(u)[-1] + 1, 0:2 * C].rearrange("p t (g d) -> p t g d", d=D)
                for side in range(2):
                    last = dve.tensor_tensor(qkn[k][:, :, :, side], src,
                                             rqk[k][:].unsqueeze(3).to_broadcast([P, HT, 2 * H, D]), ALU.mult)
                last.then_inc(qkn_made, 1)

            def KL_(u, n):
                dve.wait_ge(KS_made, u + 1)
                up = KS[u // 2 % 2][D:2 * D, :, cols_of(u)]
                dve.scalar_tensor_tensor(up, ring("kT", u, 0)[D:2 * D].rearrange("p (h s) -> p h s", h=H),
                                         gain[D:2 * D, 0:1], up.bitcast(F32), ALU.mult,
                                         ALU.subtract).then_inc(KL_made, 1)

            def QL_(u, n):
                i = u // 2
                dve.wait_ge(QH_made, u + 1)
                dve.tensor_tensor(QL[i % 2][:, :, cols_of(u)], ring("qT", u, 0)[:].rearrange("p (h s) -> p h s", h=H),
                                  QH[i % 2][:, :, cols_of(u)].bitcast(F32), ALU.subtract).then_inc(QL_made, 1)

            def ctx_stats_(u, n):
                dve.wait_ge(ctx_in, 16)
                for b in range(B):
                    last = dve.bn_stats(cstat[:, b], ctx_sb[:, b])
                dve.wait_ge(dve_step, step(last))
                for b in range(B):
                    last = dve.bn_aggr(cmv[:, b], cstat[:, b])
                last.then_inc(cmv_made, 1)

            def ctx_apply_(u, n):
                dve.wait_ge(crstd_made, 1)
                for b in range(B):
                    last = dve.tensor_scalar(cxh[:, b], ctx_sb[:, b], cmv[:, b, 0:1], crstd[:, b:b + 1],
                                             ALU.subtract, ALU.mult)
                last.then_inc(cxh_made, 1)

            def ctx_ss_(u, n):
                dve.wait_ge(ckv_made, 2)
                dve.wait_ge(dve_step, step(dve.tensor_tensor(csq[:], ckv[:, :, 0:C], ckv[:, :, 0:C], ALU.mult)))
                dve.tensor_reduce(css[:], csq[:].rearrange("m b (h d) -> m (b h) d", d=D), AX.X,
                                  ALU.add).then_inc(css_made, 1)

            def ctx_kn_(u, n):
                dve.wait_ge(crk_made, 1)
                for side in range(2):
                    last = dve.tensor_tensor(ckn[:, :, :, side], ckv[:, :, 0:C].rearrange("m b (h d) -> m b h d", d=D),
                                             crk[:].rearrange("m (b h) -> m b h", b=B).unsqueeze(3).to_broadcast(
                                                 [M, B, H, D]), ALU.mult)
                last.then_inc(ckn_made, 1)

            def ctx_KL_(u, n):
                dve.wait_ge(cKS_made, n + 1)
                up = cKS[D:2 * D, 2 * n:2 * n + 2].rearrange("p b h m -> p (b h m)")
                dve.scalar_tensor_tensor(up, ring("ctx_kT", 0, n)[D:2 * D, 0:2 * H * M], gain[D:2 * D, 0:1],
                                         up.bitcast(F32), ALU.mult, ALU.subtract).then_inc(cKL_made, 1)

            def e23_(u, n):
                k = u % 2
                dve.wait_ge(probs_made, KT * u + 4)
                if u >= 2:
                    dve.wait_ge(proj_done, HT * (u - 1))
                step(dve.tensor_tensor(esum[k][:], probs[k][2][:], probs[k][3][:], ALU.add))

            def esum1_(u, n):
                dve.wait_ge(dve_step, count[0])
                dve.wait_ge(e01_made, u + 1)
                step(dve.tensor_tensor(esum[u % 2][:], esum[u % 2][:], e01[u % 2][:], ALU.add))

            def esum2_(u, n):
                k = u % 2
                dve.wait_ge(dve_step, count[0])
                dve.wait_ge(probs_made, KT * (u + 1))
                dve.tensor_tensor(esum[k][0:M], esum[k][0:M], probs[k][T][0:M], ALU.add).then_inc(esum_made, 1)

            def x2_(u, n):
                k = u % 2
                dve.wait_ge(xbo_made, u + 1)
                ps = [ring("proj", u, m)[:].rearrange("p (g c) -> p g c", c=C) for m in range(HT)]
                for m in range(HT):
                    dve.wait_ge(proj_done, HT * u + m + 1)
                    divided = step(dve.reciprocal(rden[:, m], ps[m][:, H:2 * H, 0]))
                dve.wait_ge(dve_step, divided)
                for m in range(HT):
                    added = step(dve.scalar_tensor_tensor(x2a[:, m], ps[m][:, 0], rden[:, m, 0:1], xbo[k][:, m],
                                                          ALU.mult, ALU.add))
                dve.wait_ge(dve_step, added)
                for m in range(HT):
                    dve.scalar_tensor_tensor(x2[k][:, m], ps[m][:, 1], rden[:, m, 1:2], x2a[:, m],
                                             ALU.mult, ALU.add).then_inc(x2_made, 1)

            def stats2_(u, n):
                k = u % 2
                dve.wait_ge(x2_made, HT * (u + 1))
                for m in range(HT):
                    last = dve.bn_stats(stat2[k][:, m], x2[k][:, m])
                dve.wait_ge(dve_step, step(last))
                for m in range(HT):
                    last = dve.bn_aggr(mv2[k][:, m], stat2[k][:, m])
                last.then_inc(mv2_made, 1)

            def apply2_(u, n):
                k = u % 2
                dve.wait_ge(rstd2_made, u + 1)
                if u >= 2:
                    dve.wait_ge(l2T_done, u - 1)
                for m in range(HT):
                    last = dve.tensor_scalar(l2[k][:, m], x2[k][:, m], mv2[k][:, m, 0:1], rstd2[k][:, m:m + 1],
                                             ALU.subtract, ALU.mult)
                last.then_inc(l2_made, 1)

            def logits_(u, n):
                k = u % 2
                dve.wait_ge(gate_done, u + 1)
                dve.wait_ge(bias_in, 32)
                if u >= 2:
                    dve.wait_ge(eg_made, u - 1)
                dve.tensor_tensor(lg[k][:], ring("gate", u, 0)[:, 0:N].rearrange("p (t c) -> p t c", t=HT)[:, :, 0:E],
                                  bg_b[:].unsqueeze(1).to_broadcast([P, HT, E]), ALU.add).then_inc(lg_made, 1)
                dve.wait_ge(lg_made, u + 1)
                dve.wait_ge(dve_step, step(dve.tensor_reduce(nmx[k][:], lg[k][:], AX.X, ALU.max, negate=True)))
                dve.tensor_tensor(lgs[k][:], lg[k][:], nmx[k][:].unsqueeze(2).to_broadcast([P, HT, E]),
                                  ALU.add).then_inc(lgs_made, 1)

            def top_(u, n):
                k = u % 2
                dve.wait_ge(eg_made, u + 1)
                dve.wait_ge(iota_made, 1)
                for m in range(HT):
                    last = dve.max(top[:, m], eg[k][:, m])
                maxed = step(last)
                summed = step(dve.tensor_reduce(esm[:], eg[k][:], AX.X, ALU.add))
                dve.wait_ge(dve_step, maxed)
                for m in range(HT):
                    last = dve.max_index(topi[:, m], top[:, m], eg[k][:, m])
                indexed = step(last)
                dve.wait_ge(dve_step, summed)
                inverse = step(dve.reciprocal(erc[:], esm[:]))
                dve.wait_ge(dve_step, indexed)
                numbers = step(dve.tensor_copy(topf[:], topi[:, :, 0:2]))
                dve.wait_ge(dve_step, inverse)
                step(dve.tensor_tensor(er[:], eg[k][:], erc[:].unsqueeze(2).to_broadcast([P, HT, E]), ALU.mult))
                dve.wait_ge(dve_step, numbers)
                every = iota_e[:].unsqueeze(1).to_broadcast([P, HT, E])
                step(dve.tensor_tensor(eq1[:], every, topf[:, :, 0:1].to_broadcast([P, HT, E]), ALU.is_equal))
                step(dve.tensor_tensor(eq2[:], every, topf[:, :, 1:2].to_broadcast([P, HT, E]), ALU.is_equal))
                dve.wait_ge(dve_step, count[0])
                dve.wait_ge(dve_step, step(dve.tensor_tensor(eq1[:], eq1[:], eq2[:], ALU.add)))
                if u >= 2:
                    dve.wait_ge(scaled_made, HT * (u - 1))
                    dve.wait_ge(gateT_done, u - 1)
                dve.tensor_tensor(w[k][:], er[:], eq1[:], ALU.mult).then_inc(w_made, 1)

            def wT_(u, n):
                dve.wait_ge(gateT_done, u + 1)
                dve.wait_ge(pads_zeroed, 1)
                if u >= 1:
                    dve.wait_ge(bias_done, u)
                dve.tensor_copy(wT[0:HT * E], ring("gateT", u, 0)[0:HT * E, 0:P]).then_inc(wT_made, 1)

            def x2b_(u, n):
                dve.wait_ge(bias_done, u + 1)
                dve.tensor_tensor(x2b[u % 2][:], ring("bias", u, 0)[:, 0:N].rearrange("p (t c) -> p t c", c=C),
                                  x2[u % 2][:], ALU.add).then_inc(x2b_made, 1)

            def high_(u, n):
                m = HT * u + n
                dve.wait_ge(high_done, m + 1)
                dve.wait_ge(w_made, u + 1)
                dve.wait_ge(x2b_made, u + 1)
                if m >= 2:
                    dve.wait_ge(res_made, m - 1)
                ps = ring("high", u, n)[:].rearrange("p (e c) -> p e c", e=EH)
                src = x2b[u % 2][:, n]
                for e in range(EH - 1):
                    dve.wait_ge(dve_step, step(dve.scalar_tensor_tensor(
                        part[e][:], ps[:, e], w[u % 2][:, n, EH + e:EH + e + 1], src, ALU.mult, ALU.add)))
                    src = part[e][:]
                dve.scalar_tensor_tensor(acc[m % 2][:], ps[:, EH - 1], w[u % 2][:, n, E - 1:E], src,
                                         ALU.mult, ALU.add).then_inc(acc_made, 1)

            walk("V", dict(ones=ones_, zeros=zeros_, gain=gain_, shift=shift_, mask=mask_, cbias=cbias_, weights=weights_,
                           split=split_, stats1=stats1_, apply1=apply1_, ss=ss_, qkn=qkn_, KL=KL_, QL=QL_,
                           ctx_stats=ctx_stats_, ctx_apply=ctx_apply_, ctx_ss=ctx_ss_, ctx_kn=ctx_kn_, ctx_KL=ctx_KL_,
                           e23=e23_, esum1=esum1_, esum2=esum2_, x2=x2_, stats2=stats2_, apply2=apply2_,
                           logits=logits_, top=top_, wT=wT_, x2b=x2b_, high=high_))

        @block.tensor
        def _(pe):
            def free(kind, u, n):
                if (kind, u, n) in before:
                    was, wu, wn = before[(kind, u, n)]
                    pe.wait_ge(*RELEASED[was](wu, wn))

            def three(dst, lH, lL, rH, rL):
                pe.matmul(dst, lH, rH, start=True, stop=False)
                pe.matmul(dst, lH, rL, start=False, stop=False)
                return pe.matmul(dst, lL, rH, start=False, stop=True)

            def warm_(u, n):
                pe.wait_ge(ident_made, 1)
                for _ in range(n):
                    pe.transpose(O_ps[0][:, 0:P], ident[:], ident[:])

            def weights_(u, n):
                pe.wait_ge(ident_made, 1)
                pe.wait_ge(Wlat_in, 32)
                ps = ring("weights", 0, 0)
                pe.transpose(ps[:, 0:C], Wq_sb[:], ident[:])
                for a in range(2):
                    last = pe.transpose(ps[:, (a + 1) * C:(a + 2) * C], Wlkv_sb[:, a], ident[:])
                last.then_inc(Wlat_done, 1)

            def weights2_(u, n):
                free("weights2", 0, 0)
                ps = ring("weights2", 0, 0)
                pe.wait_ge(Wo_in, 16)
                pe.wait_ge(Wctx_in, 16)
                pe.transpose(ps[:, 0:C], Wo_sb[:], ident[:])
                for a in range(2):
                    last = pe.transpose(ps[0:CX, (a + 1) * C:(a + 2) * C], Wkv_sb[:, a], ident[:])
                last.then_inc(Wctx_done, 1)

            def maskT_(u, n):
                free("maskT", 0, 0)
                pe.wait_ge(mask_made, 1)
                pe.transpose(ring("maskT", 0, 0)[0:M, 0:B], maskf[:], ident[0:B, 0:B]).then_inc(maskT_done, 1)

            def xT_(u, n):
                free("xT", u, 0)
                pe.wait_ge(xh_made, u + 1)
                for m in range(HT):
                    last = pe.transpose(ring("xT", u, 0)[:, local(m)], xh[u % 2][:, m], ident[:])
                last.then_inc(xT_done, 1)

            def qkv_(u, n):
                k = u % 2
                free("qkv", u, n)
                pe.wait_ge(lnL_made, u + 1)
                if u == 0:
                    pe.wait_ge(WqkvL_made, 1)
                three(ring("qkv", u, n)[:, 0:3 * C], lnH[k][:, local(n)], lnL[k][:, local(n)], WqkvH[:],
                      WqkvL[:]).then_inc(qkv_done, 1)

            def heads_T(kind, u, first, done):
                free(kind, u, 0)
                pe.wait_ge(qkn_made, u + 1)
                for h in range(H):
                    for m in range(HT):
                        last = pe.transpose(ring(kind, u, 0)[:, h * N + m * P:h * N + (m + 1) * P],
                                            qkn[u % 2][:, m, first + h].rearrange("p s d -> p (s d)"), ident[:])
                last.then_inc(done, 1)

            def ctxT_(u, n):
                free("ctxT", 0, 0)
                pe.wait_ge(cxh_made, 1)
                for b in range(B):
                    last = pe.transpose(ring("ctxT", 0, 0)[0:CX, b * M:(b + 1) * M], cxh[:, b], ident[0:M, 0:M])
                last.then_inc(ctxT_done, 1)

            def ctx_kv_(u, n):
                free("ctx_kv", 0, n)
                pe.wait_ge(cT_made, 1)
                pe.wait_ge(WctxT_made, 1)
                for k in range(2):
                    last = pe.matmul(ring("ctx_kv", 0, n)[0:M, k * 2 * C:(k + 1) * 2 * C], cT[:, 2 * n + k],
                                     WctxT[:], start=True, stop=True)
                last.then_inc(ckv_done, 1)

            def ctx_kT_(u, n):
                free("ctx_kT", 0, n)
                pe.wait_ge(ckn_made, 1)
                for k in range(2 * H):
                    b, h = 2 * n + k // H, k % H
                    last = pe.transpose(ring("ctx_kT", 0, n)[:, k * M:(k + 1) * M],
                                        ckn[:, b, h].rearrange("m s d -> m (s d)"), ident[0:M, 0:M])
                last.then_inc(ckT_done, 1)

            def score_(u, n):
                i = u // 2
                free("score", u, n)
                pe.wait_ge(QL_made, u + 1)
                if n < T:
                    pe.wait_ge(KL_made, 2 * i + n // HT + 1)
                else:
                    pe.wait_ge(cKL_made, i // 2 + 1)
                for h in range(H):
                    k = KS[i % 2][:, h, n * P:(n + 1) * P] if n < T else cKS[:, i, h]
                    ps = ring("score", u, n)[0:P if n < T else M, h * N:(h + 1) * N]
                    pe.matmul(ps, k, QH[i % 2][:, h, cols_of(u)], start=True, stop=False)
                    last = pe.matmul(ps, k, QL[i % 2][:, h, cols_of(u)], start=False, stop=True)
                last.then_inc(scores_done, 1)

            def value_(u, n):
                i = u // 2
                if u >= 2 and n == 0:
                    pe.wait_ge(oT_made, u - 1)
                pe.wait_ge(probs_made, KT * u + n + 1)
                for h in range(H):
                    if n < T:
                        v, p = qkv[i % 2][:, n, 2 * C + h * D:2 * C + (h + 1) * D], probs[u % 2][n][:, h]
                    else:
                        v, p = ckv[:, i, C + h * D:C + (h + 1) * D], probs[u % 2][n][0:M, h]
                    last = pe.matmul(O_ps[u % 2][h * D:(h + 1) * D, 0:N], v, p, start=(n == 0), stop=(n == KT - 1))
                if n == KT - 1:
                    last.then_inc(O_done, 1)

            def proj_(u, n):
                k = u % 2
                free("proj", u, n)
                pe.wait_ge(oT_made, u + 1)
                pe.wait_ge(WoT_made, 1)
                ps = ring("proj", u, n)
                pe.matmul(ps[:, 0:H * C], oT[k][:, local(n)], WoT[:].rearrange("p h c -> p (h c)"), start=True, stop=True)
                pe.wait_ge(esum_made, u + 1)
                pe.wait_ge(ones_made, 1)
                for h in range(H):
                    last = pe.matmul(ps[:, (H + h) * C:(H + h + 1) * C], esum[k][:, h, local(n)], ones[:],
                                     start=True, stop=True)
                last.then_inc(proj_done, 1)

            def l2T_(u, n):
                free("l2T", u, 0)
                pe.wait_ge(l2_made, u + 1)
                for m in range(HT):
                    last = pe.transpose(ring("l2T", u, 0)[:, local(m)], l2[u % 2][:, m], ident[:])
                last.then_inc(l2T_done, 1)

            def gate_(u, n):
                free("gate", u, 0)
                pe.wait_ge(l2T_made, u + 1)
                pe.wait_ge(Wg_in, 16)
                for m in range(HT):
                    last = pe.matmul(ring("gate", u, 0)[:, local(m)], l2T[u % 2][:, local(m)], Wg_sb[:],
                                     start=True, stop=True)
                last.then_inc(gate_done, 1)

            def gateT_(u, n):
                free("gateT", u, 0)
                pe.wait_ge(w_made, u + 1)
                pe.transpose(ring("gateT", u, 0)[0:HT * E, 0:P], w[u % 2][:].rearrange("p t e -> p (t e)"),
                             ident[:]).then_inc(gateT_done, 1)

            def bias_(u, n):
                free("bias", u, 0)
                pe.wait_ge(wT_made, u + 1)
                pe.wait_ge(blk_in, 16 * HT)
                pe.matmul(ring("bias", u, 0)[:, 0:N], wT[:], bias_blk[:].rearrange("p t c -> p (t c)"),
                          start=True, stop=True).then_inc(bias_done, 1)

            def experts(kind, u, n, e0, done):
                k = u % 2
                free(kind, u, n)
                pe.wait_ge(l2L_made, u + 1)
                pe.wait_ge(WeL_made, 1)
                rH, rL = (W[:, e0:e0 + EH].rearrange("p e c -> p (e c)") for W in (WeH, WeL))
                three(ring(kind, u, n)[:], l2H[k][:, local(n)], l2L[k][:, local(n)], rH, rL).then_inc(done, 1)

            walk("P", dict(warm=warm_, weights=weights_, weights2=weights2_, maskT=maskT_, xT=xT_, qkv=qkv_,
                           kT=lambda u, n: heads_T("kT", u, H, kT_done), qT=lambda u, n: heads_T("qT", u, 0, qT_done),
                           ctxT=ctxT_, ctx_kv=ctx_kv_, ctx_kT=ctx_kT_, score=score_, value=value_, proj=proj_,
                           l2T=l2T_, gate=gate_, gateT=gateT_, bias=bias_,
                           low=lambda u, n: experts("low", u, n, 0, low_done),
                           high=lambda u, n: experts("high", u, n, EH, high_done)))


_INS = ['x', 'ctx_768', 'mask_BxS2_bk0', 'L0_xattn_ln_x_g', 'L0_xattn_ln_x_b', 'L0_xattn_ln_l_g', 'L0_xattn_ln_l_b',
        'L0_xattn_qn_g', 'L0_xattn_kn_g', 'L0_xattn_Wq', 'L0_xattn_Wkv', 'L0_xattn_Wlkv', 'L0_xattn_Wo', 'L0_xattn_bo',
        'L0_ffn_W', 'L0_ffn_b', 'L0_ffn_Wg', 'L0_ffn_bg']
_OUTS = [((4, 512, 128), 'float32')]


def kernel(**inputs):
    import numpy as _np
    import concourse.bacc as _bacc
    from concourse import mybir as _mybir
    from concourse.bass_utils import run_bass_kernel_spmd as _run

    nc = _bacc.Bacc("TRN2", target_bir_lowering=False, num_devices=1)
    arrays, args = {}, []
    for name in _INS:
        a = _np.ascontiguousarray(inputs[name])
        arrays[f"in_{name}_dram"] = a
        args.append(nc.dram_tensor(f"in_{name}_dram", a.shape, _mybir.dt.from_np(a.dtype), kind="ExternalInput").ap())
    for i, (shape, dtype) in enumerate(_OUTS):
        dt = _mybir.dt.from_np(_np.dtype(dtype))
        args.append(nc.dram_tensor(f"out_{i}_dram", shape, dt, kind="ExternalOutput").ap())
    build(nc, *args)
    r = _run(nc, [arrays], core_ids=[0])
    got = tuple(r.results[0][f"out_{i}_dram"] for i in range(len(_OUTS)))
    return got[0]
```

```python
from contextlib import ExitStack

import concourse.bass as bass
from concourse import mybir

ALU = mybir.AluOpType
ACT = mybir.ActivationFunctionType
AX = mybir.AxisListType
F32 = mybir.dt.float32
F32R = mybir.dt.float32r
U32 = mybir.dt.uint32
U8 = mybir.dt.uint8

P = 128
LN_EPS = 1e-5
RMS_EPS = 1e-8
MASKED = 1e30
SAFE_EXP = 60.0
RING = 6


BEFORE = """
    V.ones 0 0   G.blanks 0 0   P.warm 0 20   V.stats1 0 0   V.stats1 1 0   G.rstd1 0 0   G.rstd1 1 0
    V.apply1 0 0   V.zeros 0 0   P.weights 0 0   V.apply1 1 0   P.xT 0 0   A.weights 0 0   P.xT 1 0   A.lnT 0 0
    V.weights 0 0   P.warm 0 14   A.lnT 1 0   G.lnL 0 0   P.weights2 0 0   G.lnL 1 0   P.qkv 0 0   P.qkv 0 1
    A.qkv 0 0   P.qkv 1 0   V.ctx_stats 0 0   A.qkv 0 1   P.qkv 1 1   A.qkv 1 0   P.warm 0 13   A.sq 0 0
    G.ctx_rstd 0 0   A.qkv 1 1   V.ss 0 0   A.sq 1 0   V.gain 0 0   V.mask 0 0   G.rqk 0 0   V.ctx_apply 0 0
    V.ss 1 0   P.ctxT 0 0   P.warm 0 9   V.shift 0 0   A.ctxT 0 0   G.rqk 1 0   A.weights2 0 0   V.qkn 0 0
    V.stats1 2 0   P.ctx_kv 0 0   A.kH 0 0   A.twin 0 0   G.rstd1 2 0   P.ctx_kv 0 1   V.qkn 1 0   A.ctx_kv 0 0
    V.kL 0 0   A.kH 1 0   P.qT 0 0   V.apply1 2 0   A.ctx_kv 0 1   V.kL 1 0   A.QH 0 0   P.xT 2 0   V.ctx_ss 0 0
    P.kT 0 0   P.warm 0 1   P.kT 1 0   A.KS 0 0   A.twin 1 0   V.QL 0 0   G.ctx_rk 0 0   A.KS 1 0   P.qT 1 0
    V.stats1 3 0   A.lnT 2 0   P.score 0 0   P.score 0 1   A.exp 0 0   G.lnL 2 0   V.ctx_kn 0 0   A.QH 1 0
    A.exp 0 1   G.rstd1 3 0   V.QL 1 0   P.qkv 2 0   A.ctx_kH 0 0   P.qkv 2 1   G.xbo 0 0   V.apply1 3 0
    A.qkv 2 0   P.score 0 2   P.warm 0 1   A.qkv 2 1   V.ctx_kL 0 0   G.e01 0 0   P.value 0 0   A.sq 2 0
    P.ctx_kT 0 0   V.ss 2 0   P.score 0 3   A.ctx_KS 0 0   P.value 0 1   A.exp 0 2   V.split 0 0   G.rqk 2 0
    P.maskT 0 0   P.score 0 4   A.exp 0 3   P.value 0 2   P.value 0 3   P.xT 3 0   V.cbias 0 0   G.e23 0 0
    V.qkn 2 0   A.exp 0 4   A.kH 2 0   P.value 0 4   A.twin 2 0   V.kL 2 0   P.ctx_kT 0 1   V.esum1 0 0
    A.oT 0 0   P.kT 2 0   A.lnT 3 0   P.qT 2 0   A.QH 2 0   G.lnL 3 0   A.ctx_KS 0 1   A.KS 2 0
"""
PERIOD = """
    P.gateT -2 0   P.low -2 0   V.esum2 -1 0   P.proj -1 0   V.stats1 3 0   A.low -2 0   V.QL 1 0   P.proj -1 1
    V.wT -2 0   G.rstd1 3 0   V.x2 -1 0   P.score 0 0   P.qkv 2 0   A.exp 0 0   G.pair -2 0   P.qkv 2 1
    A.qkv 2 0   P.score 0 1   A.qkv 2 1   V.stats2 -1 0   P.score 0 2   A.sq 2 0   P.bias -2 0   V.apply1 3 0
    G.rstd2 -1 0   A.exp 0 1   P.high -2 0   V.ss 2 0   A.exp 0 2   P.high -2 1   V.x2b -2 0   G.rqk 2 0
    V.apply2 -1 0   P.value 0 0   V.high -2 0   P.l2T -1 0   P.low -2 1   A.l2T -1 0   P.score 0 3   G.e01 0 0
    A.low -2 1   P.gate -1 0   P.value 0 1   V.qkn 2 0   A.exp 0 3   P.xT 3 0   G.l2L -1 0   P.score 0 4
    V.logits -1 0   A.kH 2 0   P.value 0 2   G.e23 0 0   V.kL 2 0   A.gexp -1 0   A.twin 2 0   P.value 0 3
    V.top -1 0   A.exp 0 4   P.qT 2 0   A.lnT 3 0   G.pair -2 1   P.kT 2 0   P.value 0 4   V.esum1 0 0
    G.xbo 0 0   A.oT 0 0   A.QH 2 0   G.res -2 0   A.KS 2 0   G.res -2 1   G.lnL 3 0
"""
AFTER = """
    P.gateT -2 0   P.low -2 0   V.esum2 -1 0   P.proj -1 0   A.low -2 0   V.wT -2 0   P.proj -1 1   V.x2 -1 0
    G.pair -2 0   P.high -2 0   P.low -2 1   P.bias -2 0   A.low -2 1   V.stats2 -1 0   P.high -2 1   V.x2b -2 0
    G.rstd2 -1 0   V.apply2 -1 0   V.high -2 0   P.l2T -1 0   A.l2T -1 0   G.l2L -1 0   P.gate -1 0   G.res -2 0
    V.logits -1 0   P.low -1 0   G.pair -2 1   A.gexp -1 0   P.high -1 0   V.top -1 0   P.low -1 1   G.res -2 1
    P.gateT -1 0   A.low -1 0   V.wT -1 0   P.bias -1 0   A.low -1 1   G.pair -1 0   P.high -1 1   V.x2b -1 0
    V.high -1 0   G.pair -1 1   G.res -1 0   G.res -1 1
"""


def schedule(units):
    steps = []
    for period in range(units + 1):
        text = (BEFORE if period == 0 else AFTER if period == units else PERIOD).split()
        while text:
            (engine, kind), unit, index = text.pop(0).split("."), period + int(text.pop(0)), int(text.pop(0))
            if 0 <= unit < units:
                steps.append((engine, kind, unit, index))
    return steps


def build(nc, x, ctx, mask, lxg, lxb, llg, llb, qng, kng, Wq, Wkv, Wlkv, Wo, bo, We, be, Wg, bg, out):
    B, S, C = x.shape
    _, M, CX = ctx.shape
    E = We.shape[0]
    D = qng.shape[0]
    H = C // D
    T = S // P
    KT = T + 1
    SCALE = float(D) ** -0.5
    EH = E // 2
    HT = T // 2
    N = HT * P
    U = 2 * B
    steps = schedule(U)

    def tiles(u):
        return range(HT * (u % 2), HT * (u % 2) + HT)

    def cols_of(u):
        return slice(N * (u % 2), N * (u % 2) + N)

    def local(n):
        return slice(n * P, (n + 1) * P)

    jobs = [(kind, u, n) for engine, kind, u, n in steps if engine == "P" and kind not in ("value", "warm")]
    slot = {job: n % RING for n, job in enumerate(jobs)}
    before = {job: jobs[n - RING] for n, job in enumerate(jobs) if n >= RING}

    with ExitStack() as st:
        def sb(name, shape, dt=F32):
            return st.enter_context(nc.sbuf_tensor(name, shape, dt))

        def two(name, shape, dt=F32):
            return [sb(f"{name}{n}", shape, dt) for n in range(2)]

        def sem(name):
            return st.enter_context(nc.semaphore(name))

        x_sb = sb("x_sb", [P, B, T, C])
        ctx_sb = sb("ctx_sb", [M, B, CX])
        mask8 = sb("mask8", [B, M], U8)
        maskf = sb("maskf", [B, M])
        ln_cols = sb("ln_cols", [P, 2])
        qk_cols = sb("qk_cols", [P, 2])
        ctx_cols = sb("ctx_cols", [CX, 2])
        bo_b = sb("bo_b", [P, C])
        bg_b = sb("bg_b", [P, E])
        gq_b = sb("gq_b", [P, D])
        gk_b = sb("gk_b", [P, D])
        Wq_sb = sb("Wq_sb", [P, C])
        Wlkv_sb = sb("Wlkv_sb", [P, 2, C])
        Wkv_sb = sb("Wkv_sb", [P, 2, CX])
        Wo_sb = sb("Wo_sb", [P, C])
        We_sb = sb("We_sb", [P, E, C])
        WeH = sb("WeH", [P, E, C], F32R)
        WeL = sb("WeL", [P, E, C], F32R)
        WqkvH = sb("WqkvH", [P, 3 * C], F32R)
        WqkvL = sb("WqkvL", [P, 3 * C], F32R)
        WctxT = sb("WctxT", [CX, 2 * C])
        WoT = sb("WoT", [P, H, C])
        Wg_sb = sb("Wg_sb", [P, P])
        bias_blk = sb("bias_blk", [P, HT, C])
        ident = sb("ident", [P, P])
        ones = sb("ones", [P, P])
        half = sb("half", [P, HT * 2 * H])
        act_warm = sb("act_warm", [P, 1])
        iota_e = sb("iota_e", [P, E])
        gain = sb("gain", [P, 1])
        gprod = sb("gprod", [P, D])
        gmax = sb("gmax", [P, 1])
        shift0 = sb("shift0", [P, 1])
        shift = sb("shift", [P, 1])
        mbias = sb("mbias", [M, B])
        cbias = sb("cbias", [M, B])
        cstat = sb("cstat", [M, B, 6])
        cmv = sb("cmv", [M, B, 2])
        cvar = sb("cvar", [M, B])
        crstd = sb("crstd", [M, B])
        cxh = sb("cxh", [M, B, CX])
        cT = sb("cT", [CX, B, M])
        ckv = sb("ckv", [M, B, 2 * C])
        csq = sb("csq", [M, B, C])
        css = sb("css", [M, B * H])
        cms = sb("cms", [M, B * H])
        crk = sb("crk", [M, B * H])
        ckn = sb("ckn", [M, B, H, D])
        cksp = sb("cksp", [M, B, H, 2, D], F32R)
        cKS = sb("cKS", [P, B, H, M], F32R)
        stat1 = two("stat1_", [P, HT, 6])
        mv1 = two("mv1_", [P, HT, 2])
        var1 = two("var1_", [P, HT])
        rstd1 = two("rstd1_", [P, HT])
        xh = two("xh", [P, HT, C])
        lnT = two("lnT", [P, N])
        lnH = two("lnH", [P, N], F32R)
        lnL = two("lnL", [P, N], F32R)
        qkv = two("qkv", [P, T, 3 * C])
        sq = two("sq", [P, HT, 2 * C])
        ss = two("ss", [P, HT, 2 * H])
        ms = two("ms", [P, HT, 2 * H])
        rqk = two("rqk", [P, HT, 2 * H])
        qkn = two("qkn", [P, HT, 2 * H, 2, D])
        ksp = two("ksp", [P, HT, H, 2, D], F32R)
        KS = two("KS", [P, H, S], F32R)
        QH = two("QH", [P, H, S], F32R)
        QL = two("QL", [P, H, S], F32R)
        probs = [[sb(f"probs{n}_{k}", [P, H, N]) for k in range(KT)] for n in range(2)]
        e01 = two("e01_", [P, H, N])
        e23 = two("e23_", [P, H, N])
        esum = two("esum", [P, H, N])
        oT = two("oT", [P, N])
        xbo = two("xbo", [P, HT, C])
        rden = sb("rden", [P, HT, H])
        x2a = sb("x2a", [P, HT, C])
        x2 = two("x2_", [P, HT, C])
        x2b = two("x2b_", [P, HT, C])
        stat2 = two("stat2_", [P, HT, 6])
        mv2 = two("mv2_", [P, HT, 2])
        var2 = two("var2_", [P, HT])
        rstd2 = two("rstd2_", [P, HT])
        l2 = two("l2_", [P, HT, C])
        l2T = two("l2T", [P, N])
        l2H = two("l2H", [P, N], F32R)
        l2L = two("l2L", [P, N], F32R)
        lg = two("lg", [P, HT, E])
        nmx = two("nmx", [P, HT])
        lgs = two("lgs", [P, HT, E])
        eg = two("eg", [P, HT, E])
        esm = sb("esm", [P, HT])
        erc = sb("erc", [P, HT])
        top = sb("top", [P, HT, 8])
        topi = sb("topi", [P, HT, 8], U32)
        topf = sb("topf", [P, HT, 2])
        eq1 = sb("eq1", [P, HT, E])
        eq2 = sb("eq2", [P, HT, E])
        er = sb("er", [P, HT, E])
        w = two("w", [P, HT, E])
        wT = sb("wT", [P, P])
        scaled = two("scaled", [P, EH, C])
        pair = sb("pair", [P, EH // 2, C])
        low = two("low", [P, C])
        acc = sb("acc", [P, HT, C])
        part = [sb(f"part{n}", [P, HT, C]) for n in range(EH - 1)]
        res = two("res", [P, HT, C])

        O_ps = [st.enter_context(nc.psum_tensor(f"O_ps{n}", [P, S], F32)) for n in range(2)]
        R_ps = [st.enter_context(nc.psum_tensor(f"R_ps{n}", [P, S], F32)) for n in range(RING)]

        def ring(kind, u, n):
            return R_ps[slot[(kind, u, n)]]

        x_in = [sem(f"x_in{n}") for n in range(B)]
        Wlat_in, Wo_in, Wctx_in, We_in, Wg_in, blk_in = (
            sem("Wlat_in"), sem("Wo_in"), sem("Wctx_in"), sem("We_in"), sem("Wg_in"), sem("blk_in"))
        ln_in, qk_in, ctx_cols_in, mask_in, gains_in, bias_in, ctx_in = (
            sem("ln_in"), sem("qk_in"), sem("ctx_cols_in"), sem("mask_in"), sem("gains_in"), sem("bias_in"), sem("ctx_in"))
        stored = [sem(f"stored{n}") for n in range(2)]
        ident_zeroed, ident_made, half_made, ones_made, iota_made = (
            sem("ident_zeroed"), sem("ident_made"), sem("half_made"), sem("ones_made"), sem("iota_made"))
        Wg_zeroed, blk_zeroed, pads_zeroed = sem("Wg_zeroed"), sem("blk_zeroed"), sem("pads_zeroed")
        mask_made, maskT_done, gain_made, shift_made, cbias_made = (
            sem("mask_made"), sem("maskT_done"), sem("gain_made"), sem("shift_made"), sem("cbias_made"))
        Wlat_done, Wctx_done = sem("Wlat_done"), sem("Wctx_done")
        WqkvH_made, WqkvL_made, WoT_made, WctxT_made = sem("WqkvH_made"), sem("WqkvL_made"), sem("WoT_made"), sem("WctxT_made")
        WeH_made, WeL_made = sem("WeH_made"), sem("WeL_made")
        cmv_made, crstd_made, cxh_made, ctxT_done, cT_made = (
            sem("cmv_made"), sem("crstd_made"), sem("cxh_made"), sem("ctxT_done"), sem("cT_made"))
        ckv_done, ckv_made, css_made, crk_made, ckn_made, ckT_done, cKS_made, ckH_made, ckL_made = (
            sem("ckv_done"), sem("ckv_made"), sem("css_made"), sem("crk_made"), sem("ckn_made"), sem("ckT_done"),
            sem("cKS_made"), sem("ckH_made"), sem("ckL_made"))
        mv1_made, rstd1_made, xh_made, xT_done, lnT_made, lnL_made = (
            sem("mv1_made"), sem("rstd1_made"), sem("xh_made"), sem("xT_done"), sem("lnT_made"), sem("lnL_made"))
        qkv_done, qkv_made, sq_made, ss_made, rqk_made, qkn_made = (
            sem("qkv_done"), sem("qkv_made"), sem("sq_made"), sem("ss_made"), sem("rqk_made"), sem("qkn_made"))
        twin_made, kT_done, qT_done, KS_made, QH_made, kH_made, kL_made, QL_made = (
            sem("twin_made"), sem("kT_done"), sem("qT_done"), sem("KS_made"), sem("QH_made"), sem("kH_made"), sem("kL_made"), sem("QL_made"))
        scores_done, probs_made, e01_made, e23_made, esum_made, O_done, oT_made = (
            sem("scores_done"), sem("probs_made"), sem("e01_made"), sem("e23_made"), sem("esum_made"), sem("O_done"), sem("oT_made"))
        xbo_made, proj_done, x2_made, mv2_made, rstd2_made, l2_made = (
            sem("xbo_made"), sem("proj_done"), sem("x2_made"), sem("mv2_made"), sem("rstd2_made"), sem("l2_made"))
        l2T_done, l2T_made, l2L_made, gate_done, lg_made, lgs_made, eg_made = (
            sem("l2T_done"), sem("l2T_made"), sem("l2L_made"), sem("gate_done"), sem("lg_made"), sem("lgs_made"), sem("eg_made"))
        w_made, gateT_done, wT_made, bias_done, x2b_made = (
            sem("w_made"), sem("gateT_done"), sem("wT_made"), sem("bias_done"), sem("x2b_made"))
        low_done, high_done, scaled_made, low_made, acc_made, res_made = (
            sem("low_done"), sem("high_done"), sem("scaled_made"), sem("low_made"), sem("acc_made"), sem("res_made"))
        dve_step, pool_step = sem("dve_step"), sem("pool_step")

        RELEASED = {
            "weights": lambda u, n: (WqkvL_made, 1),
            "weights2": lambda u, n: (WctxT_made, 1),
            "maskT": lambda u, n: (cbias_made, 1),
            "score": lambda u, n: (probs_made, KT * u + n + 1),
            "xT": lambda u, n: (lnT_made, u + 1),
            "qkv": lambda u, n: (qkv_made, HT * u + n + 1),
            "kT": lambda u, n: (KS_made, u + 1),
            "qT": lambda u, n: (QL_made, u + 1),
            "ctxT": lambda u, n: (cT_made, 1),
            "ctx_kv": lambda u, n: (ckv_made, n + 1),
            "ctx_kT": lambda u, n: (cKS_made, n + 1),
            "proj": lambda u, n: (x2_made, HT * u + n + 1),
            "l2T": lambda u, n: (l2T_made, u + 1),
            "gate": lambda u, n: (lg_made, u + 1),
            "gateT": lambda u, n: (wT_made, u + 1),
            "bias": lambda u, n: (x2b_made, u + 1),
            "low": lambda u, n: (scaled_made, HT * u + n + 1),
            "high": lambda u, n: (acc_made, HT * u + n + 1),
        }

        def row(v):
            return v.rearrange("(a d) -> a d", a=1)

        def column(v):
            return v.rearrange("(d a) -> d a", a=1)

        def walk(engine, does):
            for who, kind, u, n in steps:
                if who == engine:
                    does[kind](u, n)

        block = st.enter_context(nc.Block())

        @block.sync
        def _(sp):
            sp.dma_start(x_sb[:, 0], x[0].rearrange("(p t) c -> p t c", t=T)).then_inc(x_in[0], 16)
            for n, v in enumerate((llg, llb)):
                sp.dma_start(ln_cols[:, n:n + 1], column(v)).then_inc(ln_in, 16)
            for n, v in enumerate((qng, kng)):
                for h in range(2):
                    sp.dma_start(qk_cols[h * D:(h + 1) * D, n:n + 1], column(v)).then_inc(qk_in, 16)
            sp.dma_start(gq_b[:], row(qng).to_broadcast([P, D])).then_inc(gains_in, 16)
            sp.dma_start(gk_b[:], row(kng).to_broadcast([P, D])).then_inc(gains_in, 16)
            sp.dma_start(ctx_sb[:], ctx.rearrange("b m c -> m b c")).then_inc(ctx_in, 16)
            for n, v in enumerate((lxg, lxb)):
                sp.dma_start(ctx_cols[:, n:n + 1], column(v)).then_inc(ctx_cols_in, 16)
            sp.dma_start(x_sb[:, 1], x[1].rearrange("(p t) c -> p t c", t=T)).then_inc(x_in[1], 16)
            sp.dma_start(mask8[:], mask).then_inc(mask_in, 16)
            sp.dma_start(We_sb[:], We.rearrange("e h o -> h e o")).then_inc(We_in, 16)
            sp.dma_start(bo_b[:], row(bo).to_broadcast([P, C])).then_inc(bias_in, 16)
            sp.dma_start(bg_b[:], row(bg).to_broadcast([P, E])).then_inc(bias_in, 16)
            sp.wait_ge(Wg_zeroed, 1)
            sp.dma_start(Wg_sb[:, 0:E], Wg).then_inc(Wg_in, 16)
            sp.wait_ge(blk_zeroed, 1)
            for t in range(HT):
                sp.dma_start(bias_blk[E * t:E * (t + 1), t], be).then_inc(blk_in, 16)
            for i in range(2, B):
                sp.dma_start(x_sb[:, i], x[i].rearrange("(p t) c -> p t c", t=T)).then_inc(x_in[i], 16)
            for u in range(U):
                dst = out[u // 2].rearrange("(p t) c -> p t c", t=T)[:, tiles(u)[0]:tiles(u)[-1] + 1]
                if u < U - 1:
                    sp.wait_ge(res_made, HT * (u + 1))
                    sp.dma_start(dst, res[u % 2][:]).then_inc(stored[u % 2], 16)
                else:
                    for n in range(HT):
                        sp.wait_ge(res_made, HT * u + n + 1)
                        sp.dma_start(dst[:, n], res[u % 2][:, n]).then_inc(stored[u % 2], 16)
            sp.wait_ge(stored[0], 16 * B)
            sp.wait_ge(stored[1], 16 * (B - 1 + HT))

        @block.gpsimd
        def _(pool):
            count = [0]

            def step(ins):
                count[0] += 1
                ins.then_inc(pool_step, 1)
                pool.wait_ge(pool_step, count[0])

            pool.memset(ident[:], 0.0).then_inc(ident_zeroed, 1)
            pool.wait_ge(ident_zeroed, 1)
            pool.affine_select(out=ident[:], in_=ident[:], compare_op=ALU.not_equal, fill=1.0, base=0,
                               pattern=[[-1, P]], channel_multiplier=1).then_inc(ident_made, 1)
            pool.memset(half[:], -0.5).then_inc(half_made, 1)

            def blanks_(u, n):
                pool.memset(Wg_sb[:], 0.0).then_inc(Wg_zeroed, 1)
                pool.memset(bias_blk[:], 0.0).then_inc(blk_zeroed, 1)
                pool.iota(iota_e[:], pattern=[[1, E]], base=0, channel_multiplier=0,
                          allow_small_or_imprecise_dtypes=True).then_inc(iota_made, 1)

            def rstd1_(u, n):
                k = u % 2
                pool.wait_ge(mv1_made, u + 1)
                step(pool.tensor_scalar(var1[k][:], mv1[k][:, :, 1], 1.0 + LN_EPS, LN_EPS * LN_EPS, ALU.mult, ALU.add))
                pool.tensor_tensor(rstd1[k][:], var1[k][:], half[:, 0:HT], ALU.pow).then_inc(rstd1_made, 1)

            def lnL_(u, n):
                k = u % 2
                pool.wait_ge(lnT_made, u + 1)
                if u >= 2:
                    pool.wait_ge(qkv_done, HT * (u - 1))
                pool.tensor_tensor(lnL[k][:], lnT[k][:], lnH[k][:].bitcast(F32), ALU.subtract).then_inc(lnL_made, 1)

            def rqk_(u, n):
                k = u % 2
                pool.wait_ge(ss_made, u + 1)
                if u >= 2:
                    pool.wait_ge(qkn_made, u - 1)
                step(pool.tensor_scalar(ms[k][:], ss[k][:], 1.0 / D, RMS_EPS * RMS_EPS, ALU.mult, ALU.max))
                pool.tensor_tensor(rqk[k][:], ms[k][:], half[:].rearrange("p (t g) -> p t g", g=2 * H),
                                   ALU.pow).then_inc(rqk_made, 1)

            def ctx_rstd_(u, n):
                pool.wait_ge(cmv_made, 1)
                step(pool.tensor_scalar(cvar[:], cmv[:, :, 1], 1.0, LN_EPS, ALU.mult, ALU.add))
                pool.tensor_tensor(crstd[:], cvar[:], half[0:M, 0:B], ALU.pow).then_inc(crstd_made, 1)

            def ctx_rk_(u, n):
                pool.wait_ge(css_made, 1)
                step(pool.tensor_scalar(cms[:], css[:], 1.0 / D, RMS_EPS * RMS_EPS, ALU.mult, ALU.max))
                pool.tensor_tensor(crk[:], cms[:], half[0:M, 0:B * H], ALU.pow).then_inc(crk_made, 1)

            def e01_(u, n):
                pool.wait_ge(probs_made, KT * u + 2)
                if u >= 2:
                    pool.wait_ge(esum_made, u - 1)
                pool.tensor_tensor(e01[u % 2][:], probs[u % 2][0][:], probs[u % 2][1][:], ALU.add).then_inc(e01_made, 1)

            def e23_(u, n):
                pool.wait_ge(probs_made, KT * u + 4)
                if u >= 2:
                    pool.wait_ge(esum_made, u - 1)
                pool.tensor_tensor(e23[u % 2][:], probs[u % 2][2][:], probs[u % 2][3][:], ALU.add).then_inc(e23_made, 1)

            def xbo_(u, n):
                pool.wait_ge(bias_in, 32)
                pool.wait_ge(x_in[u // 2], 16)
                if u >= 2:
                    pool.wait_ge(x2_made, HT * (u - 1))
                pool.tensor_tensor(xbo[u % 2][:], x_sb[:, u // 2, tiles(u)[0]:tiles(u)[-1] + 1],
                                   bo_b[:].unsqueeze(1).to_broadcast([P, HT, C]), ALU.add).then_inc(xbo_made, 1)

            def rstd2_(u, n):
                k = u % 2
                pool.wait_ge(mv2_made, u + 1)
                step(pool.tensor_scalar(var2[k][:], mv2[k][:, :, 1], 1.0, LN_EPS, ALU.mult, ALU.add))
                pool.tensor_tensor(rstd2[k][:], var2[k][:], half[:, 0:HT], ALU.pow).then_inc(rstd2_made, 1)

            def l2L_(u, n):
                k = u % 2
                pool.wait_ge(l2T_made, u + 1)
                if u >= 2:
                    pool.wait_ge(low_done, HT * (u - 1))
                    pool.wait_ge(high_done, HT * (u - 1))
                pool.tensor_tensor(l2L[k][:], l2T[k][:], l2H[k][:].bitcast(F32), ALU.subtract).then_inc(l2L_made, 1)

            def pair_(u, n):
                m = HT * u + n
                pool.wait_ge(scaled_made, m + 1)
                if m >= 1:
                    pool.wait_ge(low_made, m)
                if m >= 2:
                    pool.wait_ge(res_made, m - 1)
                step(pool.tensor_tensor(pair[:], scaled[m % 2][:, 0:EH // 2], scaled[m % 2][:, EH // 2:EH], ALU.add))
                pool.tensor_tensor(low[m % 2][:], pair[:, 0], pair[:, 1], ALU.add).then_inc(low_made, 1)

            def res_(u, n):
                m = HT * u + n
                pool.wait_ge(low_made, m + 1)
                pool.wait_ge(acc_made, m + 1)
                if n == 0 and u >= 2:
                    pool.wait_ge(stored[u % 2], 16 * (u // 2))
                pool.tensor_tensor(res[u % 2][:, n], low[m % 2][:], acc[:, n], ALU.add).then_inc(res_made, 1)

            walk("G", dict(blanks=blanks_, rstd1=rstd1_, lnL=lnL_, rqk=rqk_, ctx_rstd=ctx_rstd_, ctx_rk=ctx_rk_,
                           e01=e01_, e23=e23_, xbo=xbo_, rstd2=rstd2_, l2L=l2L_, pair=pair_, res=res_))

        @block.scalar
        def _(act):
            act.dma_start(Wlkv_sb[:], Wlkv.rearrange("(a o) c -> o a c", a=2)).then_inc(Wlat_in, 16)
            act.dma_start(Wq_sb[:], Wq).then_inc(Wlat_in, 16)
            act.dma_start(Wo_sb[:], Wo).then_inc(Wo_in, 16)
            act.dma_start(Wkv_sb[:], Wkv.rearrange("(a o) c -> o a c", a=2)).then_inc(Wctx_in, 16)

            act.wait_ge(half_made, 1)
            act.activation(act_warm[:], half[:, 0:1], ACT.Exp)

            def weights_(u, n):
                act.wait_ge(Wlat_done, 1)
                act.copy(WqkvH[:], ring("weights", 0, 0)[:, 0:3 * C]).then_inc(WqkvH_made, 1)

            def weights2_(u, n):
                act.wait_ge(Wctx_done, 1)
                act.wait_ge(pads_zeroed, 1)
                for h in range(H):
                    r = slice(h * D, (h + 1) * D)
                    last = act.copy(WoT[r, h], ring("weights2", 0, 0)[r, 0:C])
                last.then_inc(WoT_made, 1)
                act.copy(WctxT[:], ring("weights2", 0, 0)[0:CX, C:3 * C]).then_inc(WctxT_made, 1)

            def lnT_(u, n):
                k = u % 2
                act.wait_ge(xT_done, u + 1)
                act.wait_ge(ln_in, 32)
                if u >= 2:
                    act.wait_ge(qkv_done, HT * (u - 1))
                    act.wait_ge(lnL_made, u - 1)
                for dst in (lnT[k], lnH[k]):
                    last = act.activation(dst[:], ring("xT", u, 0)[:, 0:N], ACT.Identity, bias=ln_cols[:, 1:2],
                                          scale=ln_cols[:, 0:1])
                last.then_inc(lnT_made, 1)

            def qkv_(u, n):
                i = u // 2
                act.wait_ge(qkv_done, HT * u + n + 1)
                if i >= 2:
                    act.wait_ge(O_done, 2 * (i - 1))
                act.copy(qkv[i % 2][:, tiles(u)[n]], ring("qkv", u, n)[:, 0:3 * C]).then_inc(qkv_made, 1)

            def sq_(u, n):
                act.wait_ge(qkv_made, HT * (u + 1))
                if u >= 2:
                    act.wait_ge(ss_made, u - 1)
                act.activation(sq[u % 2][:], qkv[u // 2 % 2][:, tiles(u)[0]:tiles(u)[-1] + 1, 0:2 * C],
                               ACT.Square).then_inc(sq_made, 1)

            def kH_(u, n):
                act.wait_ge(qkn_made, u + 1)
                if u >= 2:
                    act.wait_ge(kT_done, u - 1)
                act.copy(ksp[u % 2][:, :, :, 0], qkn[u % 2][:, :, H:2 * H, 0]).then_inc(kH_made, 1)

            def twin_(u, n):
                k = u % 2
                act.wait_ge(qkn_made, u + 1)
                if u >= 2:
                    act.wait_ge(qT_done, u - 1)
                act.copy(qkn[k][:, :, 0:H, 1], qkn[k][:, :, 0:H, 0]).then_inc(twin_made, 1)

            def KS_(u, n):
                i = u // 2
                act.wait_ge(kT_done, u + 1)
                if i >= 2:
                    act.wait_ge(scores_done, 2 * KT * (i - 1))
                act.copy(KS[i % 2][:, :, cols_of(u)],
                         ring("kT", u, 0)[:].rearrange("p (h s) -> p h s", h=H)).then_inc(KS_made, 1)

            def QH_(u, n):
                act.wait_ge(qT_done, u + 1)
                act.wait_ge(gain_made, 1)
                if u >= 4:
                    act.wait_ge(scores_done, KT * (u - 3))
                act.activation(QH[u // 2 % 2][:, :, cols_of(u)], ring("qT", u, 0)[:].rearrange("p (h s) -> p h s", h=H),
                               ACT.Identity, scale=gain[:, 0:1]).then_inc(QH_made, 1)

            def ctxT_(u, n):
                act.wait_ge(ctxT_done, 1)
                act.wait_ge(ctx_cols_in, 32)
                act.activation(cT[:].rearrange("c b m -> c (b m)"), ring("ctxT", 0, 0)[0:CX, 0:B * M], ACT.Identity,
                               bias=ctx_cols[:, 1:2], scale=ctx_cols[:, 0:1]).then_inc(cT_made, 1)

            def ctx_kv_(u, n):
                act.wait_ge(ckv_done, n + 1)
                act.copy(ckv[:, 2 * n:2 * n + 2].rearrange("m b c -> m (b c)"),
                         ring("ctx_kv", 0, n)[0:M, :]).then_inc(ckv_made, 1)

            def ctx_kH_(u, n):
                act.wait_ge(ckn_made, 1)
                act.copy(cksp[:, :, :, 0], ckn[:]).then_inc(ckH_made, 1)

            def ctx_KS_(u, n):
                act.wait_ge(ckT_done, n + 1)
                act.copy(cKS[:, 2 * n:2 * n + 2].rearrange("p b h m -> p (b h m)"),
                         ring("ctx_kT", 0, n)[:, 0:2 * H * M]).then_inc(cKS_made, 1)

            def exp_(u, n):
                k = u % 2
                act.wait_ge(scores_done, KT * u + n + 1)
                act.wait_ge(shift_made, 1)
                if u >= 2 and n == 0:
                    act.wait_ge(O_done, u - 1)
                    act.wait_ge(esum_made, u - 1)
                ps = ring("score", u, n)[:].rearrange("p (h s) -> p h s", h=H)
                if n < T:
                    last = act.activation(probs[k][n][:], ps, ACT.Exp, bias=shift[:, 0:1])
                else:
                    act.wait_ge(cbias_made, 1)
                    last = act.activation(probs[k][n][0:M], ps[0:M], ACT.Exp, bias=cbias[:, u // 2:u // 2 + 1])
                last.then_inc(probs_made, 1)

            def oT_(u, n):
                act.wait_ge(O_done, u + 1)
                if u >= 2:
                    act.wait_ge(proj_done, HT * (u - 1))
                act.copy(oT[u % 2][:], O_ps[u % 2][:, 0:N]).then_inc(oT_made, 1)

            def l2T_(u, n):
                k = u % 2
                act.wait_ge(l2T_done, u + 1)
                if u >= 2:
                    act.wait_ge(gate_done, u - 1)
                    act.wait_ge(low_done, HT * (u - 1))
                    act.wait_ge(high_done, HT * (u - 1))
                    act.wait_ge(l2L_made, u - 1)
                for dst in (l2T[k], l2H[k]):
                    last = act.copy(dst[:], ring("l2T", u, 0)[:, 0:N])
                last.then_inc(l2T_made, 1)

            def gexp_(u, n):
                act.wait_ge(lgs_made, u + 1)
                if u >= 2:
                    act.wait_ge(w_made, u - 1)
                act.activation(eg[u % 2][:], lgs[u % 2][:], ACT.Exp).then_inc(eg_made, 1)

            def low_(u, n):
                m = HT * u + n
                act.wait_ge(low_done, m + 1)
                act.wait_ge(w_made, u + 1)
                if m >= 2:
                    act.wait_ge(low_made, m - 1)
                ps = ring("low", u, n)[:].rearrange("p (e c) -> p e c", e=EH)
                for e in range(EH):
                    last = act.activation(scaled[m % 2][:, e], ps[:, e], ACT.Copy, scale=w[u % 2][:, n, e:e + 1])
                last.then_inc(scaled_made, 1)

            walk("A", dict(weights=weights_, weights2=weights2_, lnT=lnT_, qkv=qkv_, sq=sq_, kH=kH_, twin=twin_, KS=KS_, QH=QH_,
                           ctxT=ctxT_, ctx_kv=ctx_kv_, ctx_kH=ctx_kH_, ctx_KS=ctx_KS_, exp=exp_, oT=oT_, l2T=l2T_, gexp=gexp_, low=low_))

        @block.vector
        def _(dve):
            count = [0]

            def step(ins):
                count[0] += 1
                ins.then_inc(dve_step, 1)
                return count[0]

            def ones_(u, n):
                dve.memset(ones[:], 1.0).then_inc(ones_made, 1)

            def zeros_(u, n):
                dve.memset(WoT[:], 0.0)
                dve.memset(wT[:], 0.0).then_inc(pads_zeroed, 1)

            def gain_(u, n):
                dve.wait_ge(qk_in, 64)
                dve.scalar_tensor_tensor(gain[:], qk_cols[:, 0:1], SCALE, qk_cols[:, 1:2], ALU.mult,
                                         ALU.mult).then_inc(gain_made, 1)

            def shift_(u, n):
                dve.wait_ge(gains_in, 32)
                dve.wait_ge(dve_step, step(dve.tensor_tensor(gprod[:], gq_b[:], gk_b[:], ALU.mult)))
                dve.wait_ge(dve_step, step(dve.tensor_reduce(gmax[:], gprod[:], AX.X, ALU.max, apply_absolute_value=True)))
                dve.wait_ge(dve_step, step(dve.tensor_scalar(shift0[:], gmax[:], -D * SCALE, SAFE_EXP, ALU.mult, ALU.add)))
                dve.tensor_scalar(shift[:], shift0[:], 0.0, None, ALU.min).then_inc(shift_made, 1)

            def mask_(u, n):
                dve.wait_ge(mask_in, 16)
                dve.tensor_copy(maskf[:], mask8[:]).then_inc(mask_made, 1)

            def cbias_(u, n):
                dve.wait_ge(maskT_done, 1)
                dve.wait_ge(dve_step, step(dve.tensor_scalar(mbias[:], ring("maskT", 0, 0)[0:M, 0:B], 1.0, MASKED,
                                                             ALU.subtract, ALU.mult)))
                dve.wait_ge(shift_made, 1)
                dve.tensor_scalar(cbias[:], mbias[:], shift[0:M, 0:1], None, ALU.add).then_inc(cbias_made, 1)

            def weights_(u, n):
                dve.wait_ge(WqkvH_made, 1)
                dve.tensor_tensor(WqkvL[:], ring("weights", 0, 0)[:, 0:3 * C], WqkvH[:].bitcast(F32),
                                  ALU.subtract).then_inc(WqkvL_made, 1)

            def split_(u, n):
                dve.wait_ge(We_in, 16)
                dve.tensor_copy(WeH[:], We_sb[:]).then_inc(WeH_made, 1)
                dve.wait_ge(WeH_made, 1)
                dve.tensor_tensor(WeL[:], We_sb[:], WeH[:].bitcast(F32), ALU.subtract).then_inc(WeL_made, 1)

            def stats1_(u, n):
                k = u % 2
                dve.wait_ge(x_in[u // 2], 16)
                for m, t in enumerate(tiles(u)):
                    last = dve.bn_stats(stat1[k][:, m], x_sb[:, u // 2, t])
                dve.wait_ge(dve_step, step(last))
                for m in range(HT):
                    last = dve.bn_aggr(mv1[k][:, m], stat1[k][:, m])
                last.then_inc(mv1_made, 1)

            def apply1_(u, n):
                k = u % 2
                dve.wait_ge(rstd1_made, u + 1)
                if u >= 2:
                    dve.wait_ge(xT_done, u - 1)
                for m, t in enumerate(tiles(u)):
                    last = dve.tensor_scalar(xh[k][:, m], x_sb[:, u // 2, t], mv1[k][:, m, 0:1], rstd1[k][:, m:m + 1],
                                             ALU.subtract, ALU.mult)
                last.then_inc(xh_made, 1)

            def ss_(u, n):
                k = u % 2
                dve.wait_ge(sq_made, u + 1)
                if u >= 2:
                    dve.wait_ge(rqk_made, u - 1)
                dve.tensor_reduce(ss[k][:], sq[k][:].rearrange("p t (g d) -> p t g d", d=D), AX.X,
                                  ALU.add).then_inc(ss_made, 1)

            def qkn_(u, n):
                k = u % 2
                dve.wait_ge(rqk_made, u + 1)
                if u >= 2:
                    dve.wait_ge(kT_done, u - 1)
                    dve.wait_ge(qT_done, u - 1)
                src = qkv[u // 2 % 2][:, tiles(u)[0]:tiles(u)[-1] + 1, 0:2 * C].rearrange("p t (g d) -> p t g d", d=D)
                dve.tensor_tensor(qkn[k][:, :, :, 0], src, rqk[k][:].unsqueeze(3).to_broadcast([P, HT, 2 * H, D]),
                                  ALU.mult).then_inc(qkn_made, 1)

            def kL_(u, n):
                k = u % 2
                dve.wait_ge(kH_made, u + 1)
                dve.tensor_tensor(ksp[k][:, :, :, 1], qkn[k][:, :, H:2 * H, 0], ksp[k][:, :, :, 0].bitcast(F32),
                                  ALU.subtract).then_inc(kL_made, 1)

            def QL_(u, n):
                i = u // 2
                dve.wait_ge(QH_made, u + 1)
                dve.scalar_tensor_tensor(QL[i % 2][:, :, cols_of(u)],
                                         ring("qT", u, 0)[:].rearrange("p (h s) -> p h s", h=H), gain[:, 0:1],
                                         QH[i % 2][:, :, cols_of(u)].bitcast(F32), ALU.mult,
                                         ALU.subtract).then_inc(QL_made, 1)

            def ctx_stats_(u, n):
                dve.wait_ge(ctx_in, 16)
                for b in range(B):
                    last = dve.bn_stats(cstat[:, b], ctx_sb[:, b])
                dve.wait_ge(dve_step, step(last))
                for b in range(B):
                    last = dve.bn_aggr(cmv[:, b], cstat[:, b])
                last.then_inc(cmv_made, 1)

            def ctx_apply_(u, n):
                dve.wait_ge(crstd_made, 1)
                for b in range(B):
                    last = dve.tensor_scalar(cxh[:, b], ctx_sb[:, b], cmv[:, b, 0:1], crstd[:, b:b + 1],
                                             ALU.subtract, ALU.mult)
                last.then_inc(cxh_made, 1)

            def ctx_ss_(u, n):
                dve.wait_ge(ckv_made, 2)
                dve.wait_ge(dve_step, step(dve.tensor_tensor(csq[:], ckv[:, :, 0:C], ckv[:, :, 0:C], ALU.mult)))
                dve.tensor_reduce(css[:], csq[:].rearrange("m b (h d) -> m (b h) d", d=D), AX.X,
                                  ALU.add).then_inc(css_made, 1)

            def ctx_kn_(u, n):
                dve.wait_ge(crk_made, 1)
                dve.tensor_tensor(ckn[:], ckv[:, :, 0:C].rearrange("m b (h d) -> m b h d", d=D),
                                  crk[:].rearrange("m (b h) -> m b h", b=B).unsqueeze(3).to_broadcast([M, B, H, D]),
                                  ALU.mult).then_inc(ckn_made, 1)

            def ctx_kL_(u, n):
                dve.wait_ge(ckH_made, 1)
                dve.tensor_tensor(cksp[:, :, :, 1], ckn[:], cksp[:, :, :, 0].bitcast(F32),
                                  ALU.subtract).then_inc(ckL_made, 1)

            def esum1_(u, n):
                k = u % 2
                dve.wait_ge(e01_made, u + 1)
                dve.wait_ge(e23_made, u + 1)
                if u >= 2:
                    dve.wait_ge(proj_done, HT * (u - 1))
                step(dve.tensor_tensor(esum[k][:], e01[k][:], e23[k][:], ALU.add))

            def esum2_(u, n):
                k = u % 2
                dve.wait_ge(dve_step, count[0])
                dve.wait_ge(probs_made, KT * (u + 1))
                dve.tensor_tensor(esum[k][0:M], esum[k][0:M], probs[k][T][0:M], ALU.add).then_inc(esum_made, 1)

            def x2_(u, n):
                k = u % 2
                dve.wait_ge(xbo_made, u + 1)
                ps = [ring("proj", u, m)[:].rearrange("p (g c) -> p g c", c=C) for m in range(HT)]
                for m in range(HT):
                    dve.wait_ge(proj_done, HT * u + m + 1)
                    divided = step(dve.reciprocal(rden[:, m], ps[m][:, H:2 * H, 0]))
                dve.wait_ge(dve_step, divided)
                for m in range(HT):
                    added = step(dve.scalar_tensor_tensor(x2a[:, m], ps[m][:, 0], rden[:, m, 0:1], xbo[k][:, m],
                                                          ALU.mult, ALU.add))
                dve.wait_ge(dve_step, added)
                for m in range(HT):
                    dve.scalar_tensor_tensor(x2[k][:, m], ps[m][:, 1], rden[:, m, 1:2], x2a[:, m],
                                             ALU.mult, ALU.add).then_inc(x2_made, 1)

            def stats2_(u, n):
                k = u % 2
                dve.wait_ge(x2_made, HT * (u + 1))
                for m in range(HT):
                    last = dve.bn_stats(stat2[k][:, m], x2[k][:, m])
                dve.wait_ge(dve_step, step(last))
                for m in range(HT):
                    last = dve.bn_aggr(mv2[k][:, m], stat2[k][:, m])
                last.then_inc(mv2_made, 1)

            def apply2_(u, n):
                k = u % 2
                dve.wait_ge(rstd2_made, u + 1)
                if u >= 2:
                    dve.wait_ge(l2T_done, u - 1)
                for m in range(HT):
                    last = dve.tensor_scalar(l2[k][:, m], x2[k][:, m], mv2[k][:, m, 0:1], rstd2[k][:, m:m + 1],
                                             ALU.subtract, ALU.mult)
                last.then_inc(l2_made, 1)

            def logits_(u, n):
                k = u % 2
                dve.wait_ge(gate_done, u + 1)
                dve.wait_ge(bias_in, 32)
                if u >= 2:
                    dve.wait_ge(eg_made, u - 1)
                dve.tensor_tensor(lg[k][:], ring("gate", u, 0)[:, 0:N].rearrange("p (t c) -> p t c", t=HT)[:, :, 0:E],
                                  bg_b[:].unsqueeze(1).to_broadcast([P, HT, E]), ALU.add).then_inc(lg_made, 1)
                dve.wait_ge(lg_made, u + 1)
                dve.wait_ge(dve_step, step(dve.tensor_reduce(nmx[k][:], lg[k][:], AX.X, ALU.max, negate=True)))
                dve.tensor_tensor(lgs[k][:], lg[k][:], nmx[k][:].unsqueeze(2).to_broadcast([P, HT, E]),
                                  ALU.add).then_inc(lgs_made, 1)

            def top_(u, n):
                k = u % 2
                dve.wait_ge(eg_made, u + 1)
                dve.wait_ge(iota_made, 1)
                for m in range(HT):
                    last = dve.max(top[:, m], eg[k][:, m])
                maxed = step(last)
                summed = step(dve.tensor_reduce(esm[:], eg[k][:], AX.X, ALU.add))
                dve.wait_ge(dve_step, maxed)
                for m in range(HT):
                    last = dve.max_index(topi[:, m], top[:, m], eg[k][:, m])
                indexed = step(last)
                dve.wait_ge(dve_step, summed)
                inverse = step(dve.reciprocal(erc[:], esm[:]))
                dve.wait_ge(dve_step, indexed)
                numbers = step(dve.tensor_copy(topf[:], topi[:, :, 0:2]))
                dve.wait_ge(dve_step, inverse)
                step(dve.tensor_tensor(er[:], eg[k][:], erc[:].unsqueeze(2).to_broadcast([P, HT, E]), ALU.mult))
                dve.wait_ge(dve_step, numbers)
                every = iota_e[:].unsqueeze(1).to_broadcast([P, HT, E])
                step(dve.tensor_tensor(eq1[:], every, topf[:, :, 0:1].to_broadcast([P, HT, E]), ALU.is_equal))
                step(dve.tensor_tensor(eq2[:], every, topf[:, :, 1:2].to_broadcast([P, HT, E]), ALU.is_equal))
                dve.wait_ge(dve_step, count[0])
                dve.wait_ge(dve_step, step(dve.tensor_tensor(eq1[:], eq1[:], eq2[:], ALU.add)))
                if u >= 2:
                    dve.wait_ge(scaled_made, HT * (u - 1))
                    dve.wait_ge(gateT_done, u - 1)
                dve.tensor_tensor(w[k][:], er[:], eq1[:], ALU.mult).then_inc(w_made, 1)

            def wT_(u, n):
                dve.wait_ge(gateT_done, u + 1)
                dve.wait_ge(pads_zeroed, 1)
                if u >= 1:
                    dve.wait_ge(bias_done, u)
                dve.tensor_copy(wT[0:HT * E], ring("gateT", u, 0)[0:HT * E, 0:P]).then_inc(wT_made, 1)

            def x2b_(u, n):
                dve.wait_ge(bias_done, u + 1)
                dve.tensor_tensor(x2b[u % 2][:], ring("bias", u, 0)[:, 0:N].rearrange("p (t c) -> p t c", c=C),
                                  x2[u % 2][:], ALU.add).then_inc(x2b_made, 1)

            def high_(u, n):
                k = u % 2
                dve.wait_ge(w_made, u + 1)
                dve.wait_ge(x2b_made, u + 1)
                if u >= 1:
                    dve.wait_ge(res_made, HT * u)
                src = [x2b[k][:, m] for m in range(HT)]
                summed = [0] * HT
                for e in range(EH):
                    for m in range(HT):
                        if e == 0:
                            dve.wait_ge(high_done, HT * u + m + 1)
                        else:
                            dve.wait_ge(dve_step, summed[m])
                        dst = part[e][:, m] if e < EH - 1 else acc[:, m]
                        last = dve.scalar_tensor_tensor(dst, ring("high", u, m)[:, e * C:(e + 1) * C],
                                                        w[k][:, m, EH + e:EH + e + 1], src[m], ALU.mult, ALU.add)
                        if e < EH - 1:
                            summed[m] = step(last)
                            src[m] = dst
                        else:
                            last.then_inc(acc_made, 1)

            walk("V", dict(ones=ones_, zeros=zeros_, gain=gain_, shift=shift_, mask=mask_, cbias=cbias_, weights=weights_,
                           split=split_, stats1=stats1_, apply1=apply1_, ss=ss_, qkn=qkn_, kL=kL_, QL=QL_,
                           ctx_stats=ctx_stats_, ctx_apply=ctx_apply_, ctx_ss=ctx_ss_, ctx_kn=ctx_kn_, ctx_kL=ctx_kL_,
                           esum1=esum1_, esum2=esum2_, x2=x2_, stats2=stats2_, apply2=apply2_,
                           logits=logits_, top=top_, wT=wT_, x2b=x2b_, high=high_))

        @block.tensor
        def _(pe):
            def free(kind, u, n):
                if (kind, u, n) in before:
                    was, wu, wn = before[(kind, u, n)]
                    pe.wait_ge(*RELEASED[was](wu, wn))

            def three(dst, lH, lL, rH, rL):
                pe.matmul(dst, lH, rH, start=True, stop=False)
                pe.matmul(dst, lH, rL, start=False, stop=False)
                return pe.matmul(dst, lL, rH, start=False, stop=True)

            def warm_(u, n):
                pe.wait_ge(ident_made, 1)
                for _ in range(n):
                    pe.transpose(O_ps[0][:, 0:P], ident[:], ident[:])

            def weights_(u, n):
                pe.wait_ge(ident_made, 1)
                pe.wait_ge(Wlat_in, 32)
                ps = ring("weights", 0, 0)
                pe.transpose(ps[:, 0:C], Wq_sb[:], ident[:])
                for a in range(2):
                    last = pe.transpose(ps[:, (a + 1) * C:(a + 2) * C], Wlkv_sb[:, a], ident[:])
                last.then_inc(Wlat_done, 1)

            def weights2_(u, n):
                free("weights2", 0, 0)
                ps = ring("weights2", 0, 0)
                pe.wait_ge(Wo_in, 16)
                pe.wait_ge(Wctx_in, 16)
                pe.transpose(ps[:, 0:C], Wo_sb[:], ident[:])
                for a in range(2):
                    last = pe.transpose(ps[0:CX, (a + 1) * C:(a + 2) * C], Wkv_sb[:, a], ident[:])
                last.then_inc(Wctx_done, 1)

            def maskT_(u, n):
                free("maskT", 0, 0)
                pe.wait_ge(mask_made, 1)
                pe.transpose(ring("maskT", 0, 0)[0:M, 0:B], maskf[:], ident[0:B, 0:B]).then_inc(maskT_done, 1)

            def xT_(u, n):
                free("xT", u, 0)
                pe.wait_ge(xh_made, u + 1)
                for m in range(HT):
                    last = pe.transpose(ring("xT", u, 0)[:, local(m)], xh[u % 2][:, m], ident[:])
                last.then_inc(xT_done, 1)

            def qkv_(u, n):
                k = u % 2
                free("qkv", u, n)
                pe.wait_ge(lnL_made, u + 1)
                if u == 0:
                    pe.wait_ge(WqkvL_made, 1)
                three(ring("qkv", u, n)[:, 0:3 * C], lnH[k][:, local(n)], lnL[k][:, local(n)], WqkvH[:],
                      WqkvL[:]).then_inc(qkv_done, 1)

            def heads_T(kind, u, src, done):
                free(kind, u, 0)
                for h in range(H):
                    for m in range(HT):
                        last = pe.transpose(ring(kind, u, 0)[:, h * N + m * P:h * N + (m + 1) * P],
                                            src[:, m, h].rearrange("p s d -> p (s d)"), ident[:])
                last.then_inc(done, 1)

            def kT_(u, n):
                pe.wait_ge(kL_made, u + 1)
                heads_T("kT", u, ksp[u % 2][:].bitcast(F32), kT_done)

            def qT_(u, n):
                pe.wait_ge(twin_made, u + 1)
                heads_T("qT", u, qkn[u % 2], qT_done)

            def ctxT_(u, n):
                free("ctxT", 0, 0)
                pe.wait_ge(cxh_made, 1)
                for b in range(B):
                    last = pe.transpose(ring("ctxT", 0, 0)[0:CX, b * M:(b + 1) * M], cxh[:, b], ident[0:M, 0:M])
                last.then_inc(ctxT_done, 1)

            def ctx_kv_(u, n):
                free("ctx_kv", 0, n)
                pe.wait_ge(cT_made, 1)
                pe.wait_ge(WctxT_made, 1)
                for k in range(2):
                    last = pe.matmul(ring("ctx_kv", 0, n)[0:M, k * 2 * C:(k + 1) * 2 * C], cT[:, 2 * n + k],
                                     WctxT[:], start=True, stop=True)
                last.then_inc(ckv_done, 1)

            def ctx_kT_(u, n):
                free("ctx_kT", 0, n)
                pe.wait_ge(ckL_made, 1)
                for k in range(2 * H):
                    b, h = 2 * n + k // H, k % H
                    last = pe.transpose(ring("ctx_kT", 0, n)[:, k * M:(k + 1) * M],
                                        cksp[:, b, h].rearrange("m s d -> m (s d)").bitcast(F32), ident[0:M, 0:M])
                last.then_inc(ckT_done, 1)

            def score_(u, n):
                i = u // 2
                free("score", u, n)
                pe.wait_ge(QL_made, u + 1)
                if n < T:
                    pe.wait_ge(KS_made, 2 * i + n // HT + 1)
                else:
                    pe.wait_ge(cKS_made, i // 2 + 1)
                for h in range(H):
                    k = KS[i % 2][:, h, n * P:(n + 1) * P] if n < T else cKS[:, i, h]
                    ps = ring("score", u, n)[0:P if n < T else M, h * N:(h + 1) * N]
                    pe.matmul(ps, k, QH[i % 2][:, h, cols_of(u)], start=True, stop=False)
                    last = pe.matmul(ps, k, QL[i % 2][:, h, cols_of(u)], start=False, stop=True)
                last.then_inc(scores_done, 1)

            def value_(u, n):
                i = u // 2
                if u >= 2 and n == 0:
                    pe.wait_ge(oT_made, u - 1)
                pe.wait_ge(probs_made, KT * u + n + 1)
                for h in range(H):
                    if n < T:
                        v, p = qkv[i % 2][:, n, 2 * C + h * D:2 * C + (h + 1) * D], probs[u % 2][n][:, h]
                    else:
                        v, p = ckv[:, i, C + h * D:C + (h + 1) * D], probs[u % 2][n][0:M, h]
                    last = pe.matmul(O_ps[u % 2][h * D:(h + 1) * D, 0:N], v, p, start=(n == 0), stop=(n == KT - 1))
                if n == KT - 1:
                    last.then_inc(O_done, 1)

            def proj_(u, n):
                k = u % 2
                free("proj", u, n)
                pe.wait_ge(oT_made, u + 1)
                pe.wait_ge(WoT_made, 1)
                ps = ring("proj", u, n)
                pe.matmul(ps[:, 0:H * C], oT[k][:, local(n)], WoT[:].rearrange("p h c -> p (h c)"), start=True, stop=True)
                pe.wait_ge(esum_made, u + 1)
                pe.wait_ge(ones_made, 1)
                for h in range(H):
                    last = pe.matmul(ps[:, (H + h) * C:(H + h + 1) * C], esum[k][:, h, local(n)], ones[:],
                                     start=True, stop=True)
                last.then_inc(proj_done, 1)

            def l2T_(u, n):
                free("l2T", u, 0)
                pe.wait_ge(l2_made, u + 1)
                for m in range(HT):
                    last = pe.transpose(ring("l2T", u, 0)[:, local(m)], l2[u % 2][:, m], ident[:])
                last.then_inc(l2T_done, 1)

            def gate_(u, n):
                free("gate", u, 0)
                pe.wait_ge(l2T_made, u + 1)
                pe.wait_ge(Wg_in, 16)
                for m in range(HT):
                    last = pe.matmul(ring("gate", u, 0)[:, local(m)], l2T[u % 2][:, local(m)], Wg_sb[:],
                                     start=True, stop=True)
                last.then_inc(gate_done, 1)

            def gateT_(u, n):
                free("gateT", u, 0)
                pe.wait_ge(w_made, u + 1)
                pe.transpose(ring("gateT", u, 0)[0:HT * E, 0:P], w[u % 2][:].rearrange("p t e -> p (t e)"),
                             ident[:]).then_inc(gateT_done, 1)

            def bias_(u, n):
                free("bias", u, 0)
                pe.wait_ge(wT_made, u + 1)
                pe.wait_ge(blk_in, 16 * HT)
                pe.matmul(ring("bias", u, 0)[:, 0:N], wT[:], bias_blk[:].rearrange("p t c -> p (t c)"),
                          start=True, stop=True).then_inc(bias_done, 1)

            def experts(kind, u, n, e0, done):
                k = u % 2
                free(kind, u, n)
                pe.wait_ge(l2L_made, u + 1)
                pe.wait_ge(WeL_made, 1)
                rH, rL = (W[:, e0:e0 + EH].rearrange("p e c -> p (e c)") for W in (WeH, WeL))
                three(ring(kind, u, n)[:], l2H[k][:, local(n)], l2L[k][:, local(n)], rH, rL).then_inc(done, 1)

            walk("P", dict(warm=warm_, weights=weights_, weights2=weights2_, maskT=maskT_, xT=xT_, qkv=qkv_,
                           kT=kT_, qT=qT_,
                           ctxT=ctxT_, ctx_kv=ctx_kv_, ctx_kT=ctx_kT_, score=score_, value=value_, proj=proj_,
                           l2T=l2T_, gate=gate_, gateT=gateT_, bias=bias_,
                           low=lambda u, n: experts("low", u, n, 0, low_done),
                           high=lambda u, n: experts("high", u, n, EH, high_done)))


_INS = ['x', 'ctx_768', 'mask_BxS2_bk0', 'L0_xattn_ln_x_g', 'L0_xattn_ln_x_b', 'L0_xattn_ln_l_g', 'L0_xattn_ln_l_b',
        'L0_xattn_qn_g', 'L0_xattn_kn_g', 'L0_xattn_Wq', 'L0_xattn_Wkv', 'L0_xattn_Wlkv', 'L0_xattn_Wo', 'L0_xattn_bo',
        'L0_ffn_W', 'L0_ffn_b', 'L0_ffn_Wg', 'L0_ffn_bg']
_OUTS = [((4, 512, 128), 'float32')]


def kernel(**inputs):
    import numpy as _np
    import concourse.bacc as _bacc
    from concourse import mybir as _mybir
    from concourse.bass_utils import run_bass_kernel_spmd as _run

    nc = _bacc.Bacc("TRN2", target_bir_lowering=False, num_devices=1)
    arrays, args = {}, []
    for name in _INS:
        a = _np.ascontiguousarray(inputs[name])
        arrays[f"in_{name}_dram"] = a
        args.append(nc.dram_tensor(f"in_{name}_dram", a.shape, _mybir.dt.from_np(a.dtype), kind="ExternalInput").ap())
    for i, (shape, dtype) in enumerate(_OUTS):
        dt = _mybir.dt.from_np(_np.dtype(dtype))
        args.append(nc.dram_tensor(f"out_{i}_dram", shape, dt, kind="ExternalOutput").ap())
    build(nc, *args)
    r = _run(nc, [arrays], core_ids=[0])
    got = tuple(r.results[0][f"out_{i}_dram"] for i in range(len(_OUTS)))
    return got[0]
```
